# Optimizing a Trainium2 kernel written in Bass

```python
import numpy as np
import jax
import jax.numpy as jnp

def _softmax(x, axis=-1):
    return jax.nn.softmax(x, axis=axis)
def _gelu(x):
    return jax.nn.gelu(x, approximate=True)
def _silu(x):
    return jax.nn.silu(x)
def _sigmoid(x):
    return jax.nn.sigmoid(x)
def _layernorm(x, axis=-1, eps=1e-5):
    m = jnp.mean(x, axis=axis, keepdims=True)
    v = jnp.var(x, axis=axis, keepdims=True)
    return (x - m) / jnp.sqrt(v + eps)
def _scatter_add(tgt, idx, src, axis=0):
    return tgt.at[idx].add(src)
def _segment_sum(src, seg, n):
    return jax.ops.segment_sum(src, seg, n)

kernel_name = 'mk_adj_ffn_d1_adj_256_57b0e8'

def setup_inputs(seed: int = 0):
    np.random.seed(seed)
    _w = jnp.asarray
    def _rec_inputs():
        import jax
        import jax.numpy as jnp
        _gk = jax.random.key(seed)
        x = -0.0002928 + 1 * jax.random.normal(jax.random.fold_in(_gk, 1), (128, 128, 256), jnp.float32)
        _a = jax.random.bernoulli(jax.random.fold_in(_gk, 2), 0.03125, (128, 128, 128))
        _a = jnp.logical_or(_a, jnp.swapaxes(_a, -1, -2))
        _a = jnp.logical_or(_a, jnp.eye(128, dtype=bool))
        _af = _a.astype(jnp.float32)
        _af = _af * jax.random.uniform(jax.random.fold_in(_gk, 3), (128, 128, 128), jnp.float32, 0.05, 1)
        adj = _af
        return x, adj
    x, adj = _rec_inputs()
    def _L0_gnn_setup():
        import jax, jax.numpy as jnp
        import numpy as np
        B, N, DIN, DOUT = (8, 2048, 256, 256)
        ALPHA = 0.2
        EPS = 1e-06
        key = jax.random.key(seed)
        k1, k2, k3, k4 = jax.random.split(key, 4)
        h = jax.random.normal(k1, (B, N, DIN), dtype=jnp.float32)
        adj = jax.random.uniform(k2, (B, N, N), dtype=jnp.float32)
        gain = 1.414
        limW = gain * np.sqrt(6.0 / (DIN + DOUT))
        W = jax.random.uniform(k3, (DIN, DOUT), minval=-limW, maxval=limW, dtype=jnp.float32)
        lima = gain * np.sqrt(6.0 / (2 * DOUT + 1))
        a = jax.random.uniform(k4, (2 * DOUT, 1), minval=-lima, maxval=lima, dtype=jnp.float32)
        return {'h': h, 'adj': adj, 'W': W, 'a': a}
    _L0_gnn_all = _L0_gnn_setup()
    _L0_gnn_in = {k: v for k, v in _L0_gnn_all.items() if k in ('W', 'a', )}
    del _L0_gnn_all

    def _L0_ffn_setup():
        import jax, jax.numpy as jnp
        import numpy as np
        BN_EPS = 0.001

        def _bn(h, g, b, m, v):
            return g * (h - m) * jax.lax.rsqrt(v + BN_EPS) + b
        key = jax.random.key(seed)
        ks = jax.random.split(key, 8)
        B, F, Df = (256, 64, 256)
        E, H, D = (8, 256, 256)
        s1 = 1.0 / np.sqrt(Df)
        s2 = 1.0 / np.sqrt(H)
        return {'x': jax.random.normal(ks[0], (B, F, Df), jnp.float32), 'Wr': jax.random.normal(ks[1], (Df, E), jnp.float32) * s1, 'br': jnp.zeros((E,), jnp.float32), 'W1': jax.random.normal(ks[2], (E, Df, H), jnp.float32) * s1, 'b1': jnp.zeros((E, H), jnp.float32), 'g1': jnp.ones((E, H), jnp.float32), 'be1': jnp.zeros((E, H), jnp.float32), 'm1': jnp.zeros((E, H), jnp.float32), 'v1': jnp.ones((E, H), jnp.float32), 'W2': jax.random.normal(ks[3], (E, H, H), jnp.float32) * s2, 'b2': jnp.zeros((E, H), jnp.float32), 'g2': jnp.ones((E, H), jnp.float32), 'be2': jnp.zeros((E, H), jnp.float32), 'm2': jnp.zeros((E, H), jnp.float32), 'v2': jnp.ones((E, H), jnp.float32), 'Wo': jax.random.normal(ks[4], (E, H, D), jnp.float32) * s2, 'bo': jnp.zeros((E, D), jnp.float32)}
    _L0_ffn_all = _L0_ffn_setup()
    _L0_ffn_in = {k: v for k, v in _L0_ffn_all.items() if k in ('Wr', 'br', 'W1', 'b1', 'g1', 'be1', 'm1', 'v1', 'W2', 'b2', 'g2', 'be2', 'm2', 'v2', 'Wo', 'bo', )}
    del _L0_ffn_all

    return {
        "x": x,
        "adj": adj,
        "L0_gnn_W": _L0_gnn_in["W"],
        "L0_gnn_a": _L0_gnn_in["a"],
        "L0_ffn_Wr": _L0_ffn_in["Wr"],
        "L0_ffn_br": _L0_ffn_in["br"],
        "L0_ffn_W1": _L0_ffn_in["W1"],
        "L0_ffn_b1": _L0_ffn_in["b1"],
        "L0_ffn_g1": _L0_ffn_in["g1"],
        "L0_ffn_be1": _L0_ffn_in["be1"],
        "L0_ffn_m1": _L0_ffn_in["m1"],
        "L0_ffn_v1": _L0_ffn_in["v1"],
        "L0_ffn_W2": _L0_ffn_in["W2"],
        "L0_ffn_b2": _L0_ffn_in["b2"],
        "L0_ffn_g2": _L0_ffn_in["g2"],
        "L0_ffn_be2": _L0_ffn_in["be2"],
        "L0_ffn_m2": _L0_ffn_in["m2"],
        "L0_ffn_v2": _L0_ffn_in["v2"],
        "L0_ffn_Wo": _L0_ffn_in["Wo"],
        "L0_ffn_bo": _L0_ffn_in["bo"],
    }

def reference(x, adj, L0_gnn_W, L0_gnn_a, L0_ffn_Wr, L0_ffn_br, L0_ffn_W1, L0_ffn_b1, L0_ffn_g1, L0_ffn_be1, L0_ffn_m1, L0_ffn_v1, L0_ffn_W2, L0_ffn_b2, L0_ffn_g2, L0_ffn_be2, L0_ffn_m2, L0_ffn_v2, L0_ffn_Wo, L0_ffn_bo):
    import jax
    import jax.numpy as jnp
    def _L0_gnn_ref(h, adj, W, a):
        import jax, jax.numpy as jnp
        import numpy as np
        B, N, DIN, DOUT = (8, 2048, 256, 256)
        ALPHA = 0.2
        EPS = 1e-06
        Wh = jnp.einsum('bnd,df->bnf', h, W)
        a1 = a[:DOUT, 0]
        a2 = a[DOUT:, 0]
        s1 = Wh @ a1
        s2 = Wh @ a2
        e = s1[:, :, None] + s2[:, None, :]
        e = jnp.where(e > 0, e, ALPHA * e)
        e = e + jnp.log(adj + EPS)
        alpha_w = jax.nn.softmax(e, axis=-1)
        h_prime = jnp.einsum('bij,bjf->bif', alpha_w, Wh)
        return h_prime

    def _L0_ffn_ref(x, Wr, br, W1, b1, g1, be1, m1, v1, W2, b2, g2, be2, m2, v2, Wo, bo):
        import jax, jax.numpy as jnp
        import numpy as np
        BN_EPS = 0.001

        def _bn(h, g, b, m, v):
            return g * (h - m) * jax.lax.rsqrt(v + BN_EPS) + b
        feat = jnp.mean(x, axis=0)
        w = jax.nn.softmax(feat @ Wr + br, axis=-1)
        h = jnp.einsum('bfd,edh->bfeh', x, W1) + b1
        h = jax.nn.relu(_bn(h, g1, be1, m1, v1))
        h = jnp.einsum('bfeh,ehk->bfek', h, W2) + b2
        h = jax.nn.relu(_bn(h, g2, be2, m2, v2))
        y = jnp.einsum('bfeh,ehd->bfed', h, Wo) + bo
        return jnp.einsum('bfed,fe->bfd', y, w)

    x = x + _L0_gnn_ref(_layernorm(x, axis=-1), adj, L0_gnn_W, L0_gnn_a)
    x = x + _L0_ffn_ref(_layernorm(x, axis=-1), L0_ffn_Wr, L0_ffn_br, L0_ffn_W1, L0_ffn_b1, L0_ffn_g1, L0_ffn_be1, L0_ffn_m1, L0_ffn_v1, L0_ffn_W2, L0_ffn_b2, L0_ffn_g2, L0_ffn_be2, L0_ffn_m2, L0_ffn_v2, L0_ffn_Wo, L0_ffn_bo)
    return x


_drawn_inputs = setup_inputs


def setup_inputs(seed=0):
    import zlib

    import numpy as np

    out = dict(_drawn_inputs(seed))
    spreads = {'L0_ffn_br': (0.0, 0.328),
     'L0_ffn_b1': (0.0, 0.558),
     'L0_ffn_g1': (1.0, 0.541),
     'L0_ffn_be1': (0.0, 0.576),
     'L0_ffn_m1': (0.0, 0.55),
     'L0_ffn_v1': (1.0, 0.6),
     'L0_ffn_b2': (0.0, 0.403),
     'L0_ffn_g2': (1.0, 0.2),
     'L0_ffn_be2': (0.0, 0.406),
     'L0_ffn_m2': (0.0, 0.408),
     'L0_ffn_v2': (1.0, 0.6),
     'L0_ffn_bo': (0.0, 0.298)}
    factors = {'L0_ffn_Wr': 2.917}
    for name, (base, spread) in spreads.items():
        noise = np.random.default_rng([zlib.crc32(name.encode()), seed]).standard_normal(out[name].shape)
        drawn = base * np.exp(spread * noise) if base else spread * noise
        out[name] = jnp.asarray(drawn.astype(out[name].dtype))
    for name, factor in factors.items():
        out[name] = (out[name] * factor).astype(out[name].dtype)
    return out
```

```python
from contextlib import ExitStack

import concourse.bass as bass
from concourse import mybir

F32 = mybir.dt.float32
F32R = mybir.dt.float32r
ALU = mybir.AluOpType
ACT = mybir.ActivationFunctionType
AX_X = mybir.AxisListType.X

P = 128
LN_EPS = 1e-5
ADJ_EPS = 1e-6
BN_EPS = 1e-3
SLOPE = 0.2


def wait(eng, sem, value):
    if isinstance(value, int) and value <= 0:
        return
    eng.wait_ge(sem, value)


def adj_ffn(nc, x, adj, gnn_w, gnn_a, wr, br, w1, b1, g1, be1, m1, v1, w2, b2, g2, be2, m2, v2, wo, bo, out):
    B, N, D = x.shape
    E = wr.shape[1]
    C = D // P
    GB = 4
    T = GB * N
    G = B // GB
    EC = E * C
    NW = 3 * E
    assert N == P and T == 512 and G % 2 == 0 and G >= 8

    x_g = x.rearrange("(g b) n d -> g n b d", b=GB)
    adj_g = adj.rearrange("(g b) i j -> g i b j", b=GB)
    out_g = out.rearrange("(g b) n d -> g n b d", b=GB)
    x1_dram = nc.dram_tensor("x1_scratch", (G, P, GB * D), F32, kind="Internal").ap()

    with ExitStack() as ctx:
        def sb(name, shape, dt=F32, stack=ctx):
            return stack.enter_context(nc.sbuf_tensor(name, shape, dt))

        def sem(name, stack=ctx):
            return stack.enter_context(nc.semaphore(name))

        ident = sb("ident", [P, P])
        minus_half = sb("minus_half", [P, C * P])
        ones_col = sb("ones_col", [P, 1])
        eps_cols = sb("eps_cols", [P, GB])
        minus_one = sb("minus_one", [P, GB])
        w_hi = sb("w_hi", [P, NW, C, D], F32R)
        w_lo = sb("w_lo", [P, NW, C, D], F32R)
        bn_cols = sb("bn_cols", [P, 4, EC])
        acc = sb("acc", [P, GB, D])
        wr_sb = sb("wr_sb", [P, C, E])
        br_sb = sb("br_sb", [P, E])
        bo_sb = sb("bo_sb", [E, D])

        setup_done = sem("setup_done")
        phase_a_done = sem("phase_a_done")

        with ExitStack() as sa:
            def sba(name, shape, dt=F32):
                return sb(name, shape, dt, sa)

            def ps(name, shape):
                return sa.enter_context(nc.psum_tensor(name, shape, F32))

            w_stage = sba("w_stage", [P, 4, C, D])
            bn_rows = sba("bn_rows", [EC, 2, 5, P])
            bn_tmp = sba("bn_tmp", [EC, 4, 2, P])
            bn_out = sba("bn_out", [EC, 4, P])
            a_rows = sba("a_rows", [2 * C, P])
            a_cols = sba("a_cols", [P, 2 * C])
            gw = sba("gw", [P, C, D])
            gwT = sba("gwT", [P, C, D])
            va = sba("va", [P, C, 2])
            x_sb = [sba(f"x_sb{i}", [P, GB, D]) for i in range(2)]
            res = [sba(f"res{i}", [P, GB, D]) for i in range(2)]
            adj_sb = [sba(f"adj_sb{i}", [P, GB, N]) for i in range(2)]
            st1 = sba("st1", [P, GB, 6])
            mv1 = [sba(f"mv1_{i}", [P, GB, 2]) for i in range(2)]
            ve1 = sba("ve1", [P, GB])
            rstd1 = [sba(f"rstd1_{i}", [P, GB]) for i in range(2)]
            xn = sba("xn", [P, GB, D])
            xnT = sba("xnT", [P, C, T])
            wh = [sba(f"wh{i}", [P, GB, D]) for i in range(2)]
            s_sb = [sba(f"s_sb{i}", [P, GB, 2]) for i in range(2)]
            s2max = sba("s2max", [P, GB])
            neg_u = sba("neg_u", [P, GB])
            neg_m = sba("neg_m", [P, GB])
            exp_bias = [sba(f"exp_bias{i}", [P, 2, GB]) for i in range(2)]
            e_sb = [sba(f"e_sb{i}", [P, 2, GB, N]) for i in range(2)]
            e_max = sba("e_max", [P, GB, N])
            p_sb = sba("p_sb", [P, GB, N])
            pT = sba("pT", [P, GB, N])
            rinv = sba("rinv", [P, GB])
            x1 = [sba(f"x1_{i}", [P, GB, D]) for i in range(2)]
            st2 = sba("st2", [P, GB, 6])
            mv2 = [sba(f"mv2_{i}", [P, GB, 2]) for i in range(2)]
            ve2 = sba("ve2", [P, GB])
            neg_mean2 = sba("neg_mean2", [P, GB])
            rstd2 = [sba(f"rstd2_{i}", [P, GB]) for i in range(2)]
            nb2 = [sba(f"nb2_{i}", [P, GB]) for i in range(2)]
            xn2 = [sba(f"xn2_{i}", [P, GB, D]) for i in range(2)]

            ps_xT = ps("ps_xT", [P, C, T])
            ps_wh = ps("ps_wh", [P, GB, D])
            ps_pT = ps("ps_pT", [P, GB, N])
            ps_h = ps("ps_h", [P, GB, D])
            ps_s = ps("ps_s", [P, GB, N])
            ps_cols = ps_s[:, 0, 0:2 * GB].rearrange("p (b k) -> p b k", k=2)
            ps_rowsum = ps_pT[:, 0, 0:GB]

            w_loaded = [sem(f"w_loaded{i}", sa) for i in range(4)]
            w_hi_done = sem("w_hi_done", sa)
            w_lo_done = sem("w_lo_done", sa)
            small_loaded = sem("small_loaded", sa)
            bn_step = sem("bn_step", sa)
            bn_rows_done = sem("bn_rows_done", sa)
            setup_T = sem("setup_T", sa)
            setup_copied = sem("setup_copied", sa)
            x_loaded = [sem(f"x_loaded{i}", sa) for i in range(2)]
            res_loaded = [sem(f"res_loaded{i}", sa) for i in range(2)]
            adj_loaded = [sem(f"adj_loaded{i}", sa) for i in range(2)]
            bnst1 = sem("bnst1", sa)
            stats1_done = sem("stats1_done", sa)
            ve1_done = sem("ve1_done", sa)
            rstd1_done = sem("rstd1_done", sa)
            xn_done = sem("xn_done", sa)
            xT_ready = sem("xT_ready", sa)
            xT_copied = sem("xT_copied", sa)
            wh_ready = sem("wh_ready", sa)
            wh_copied = sem("wh_copied", sa)
            s_ready = sem("s_ready", sa)
            s_copied = sem("s_copied", sa)
            s2b_ready = sem("s2b_ready", sa)
            s2max_done = sem("s2max_done", sa)
            neg_u_done = sem("neg_u_done", sa)
            neg_m_done = sem("neg_m_done", sa)
            bias_done = sem("bias_done", sa)
            e_max_done = sem("e_max_done", sa)
            e_done = sem("e_done", sa)
            p_done = sem("p_done", sa)
            pT_ready = sem("pT_ready", sa)
            pT_copied = sem("pT_copied", sa)
            h_ready = sem("h_ready", sa)
            rinv_done = sem("rinv_done", sa)
            x1_done = sem("x1_done", sa)
            x1_stored = [sem(f"x1_stored{i}", sa) for i in range(2)]
            bnst2 = sem("bnst2", sa)
            stats2_done = sem("stats2_done", sa)
            ve2_done = sem("ve2_done", sa)
            rstd2_done = sem("rstd2_done", sa)
            nb2_done = sem("nb2_done", sa)
            xn2_done = sem("xn2_done", sa)
            acc_done = sem("acc_done", sa)
            N_SMALL = 10 + 5

            w_dram = [w.rearrange("e (c p) n -> e p c n", p=P) for w in (w1, w2, wo)]

            def num(g):
                return 2 * g[0] + g[1]

            def ago(g, n):
                q = g[1] - n
                return (g[0] + q // 2, q % 2)

            def exists(g):
                return not isinstance(g[0], int) or 0 <= num(g) < G

            def over_groups(eng, step):
                for i in range(4):
                    step((i // 2, i % 2))
                with eng.Fori(2, G // 2 - 1) as k:
                    step((k, 0))
                    step((k, 1))
                for i in range(G - 2, G + 2):
                    step((i // 2, i % 2))

            block = sa.enter_context(nc.Block())

            @block.sync
            def _(sp):
                def load_x(g):
                    p = g[1]
                    wait(sp, xn_done, num(g) - 1)
                    sp.dma_start(x_sb[p][:, :, :], x_g[num(g)]).then_inc(x_loaded[p], 16)

                load_x((0, 0))
                load_x((0, 1))
                sp.dma_start(gw[:, :, :], gnn_w.rearrange("(c p) n -> p c n", p=P)).then_inc(small_loaded, 16)
                sp.dma_start(a_rows[:, :], gnn_a.rearrange("(r p) o -> r (p o)", p=P)).then_inc(small_loaded, 16)
                sp.dma_start(wr_sb[:, :, :], wr.rearrange("(c p) e -> p c e", p=P)).then_inc(small_loaded, 16)
                sp.dma_start(br_sb[:, :], br.partition_broadcast(P)).then_inc(small_loaded, 16)
                sp.dma_start(bo_sb[:, :], bo).then_inc(small_loaded, 16)
                for layer, rows in enumerate(((g1, b1, be1, m1, v1), (g2, b2, be2, m2, v2))):
                    for i, r in enumerate(rows):
                        sp.dma_start(bn_rows[:, layer, i, :],
                                     r.rearrange("e (c p) -> (e c) p", p=P)).then_inc(small_loaded, 16)
                for i in range(NW):
                    wait(sp, w_lo_done, i - 3)
                    sp.dma_start(w_stage[:, i % 4, :, :], w_dram[i // E][i % E]).then_inc(w_loaded[i % 4], 16)

                def step(g):
                    p = g[1]
                    if exists(g):
                        wait(sp, p_done, num(g) - 1)
                        sp.dma_start(adj_sb[p][:, :, :], adj_g[num(g)]).then_inc(adj_loaded[p], 16)
                        wait(sp, x1_done, num(g) - 1)
                        sp.dma_start(res[p][:, :, :], x_g[num(g)]).then_inc(res_loaded[p], 16)
                    if exists(ago(g, -2)):
                        load_x(ago(g, -2))
                    b = ago(g, 1)
                    if exists(b):
                        wait(sp, x1_done, num(b) + 1)
                        sp.dma_start(x1_dram[num(b)], x1[b[1]][:, :, :].rearrange("p b d -> p (b d)")
                                     ).then_inc(x1_stored[b[1]], 16)

                over_groups(sp, step)
                for p in range(2):
                    sp.wait_ge(x1_stored[p], 16 * (G // 2))

            @block.gpsimd
            def _(pool):
                nc.gpsimd.memset(ident[:, :], 0.0).then_inc(bn_step, 1)
                nc.gpsimd.memset(minus_half[:, :], -0.5)
                nc.gpsimd.memset(ones_col[:, :], 1.0)
                nc.gpsimd.memset(eps_cols[:, :], LN_EPS)
                nc.gpsimd.memset(minus_one[:, :], -1.0)
                nc.gpsimd.memset(acc[:, :, :], 0.0)
                pool.wait_ge(bn_step, 1)
                nc.gpsimd.affine_select(out=ident[:, :], in_=ident[:, :], compare_op=ALU.not_equal, fill=1.0,
                                        base=0, pattern=[[-1, P]], channel_multiplier=1).then_inc(setup_done, 1)
                pool.wait_ge(setup_done, 1)

                def rstd_1(g):
                    p = g[1]
                    pool.wait_ge(stats1_done, num(g) + 1)
                    nc.gpsimd.tensor_tensor(ve1[:, :], mv1[p][:, :, 1], eps_cols[:, :], ALU.add).then_inc(ve1_done, 1)
                    pool.wait_ge(ve1_done, num(g) + 1)
                    nc.gpsimd.tensor_tensor(rstd1[p][:, :], ve1[:, :], minus_half[:, 0:GB],
                                            ALU.pow).then_inc(rstd1_done, 1)

                rstd_1((0, 0))
                pool.wait_ge(small_loaded, 16 * N_SMALL)
                exps = minus_half[0:EC, 0:2 * P].rearrange("p (l n) -> p l n", l=2)
                nc.gpsimd.tensor_scalar(bn_tmp[:, 0], bn_rows[:, :, 4, :], BN_EPS, None, ALU.add).then_inc(bn_step, 1)
                nc.gpsimd.tensor_tensor(bn_tmp[:, 2], bn_rows[:, :, 1, :], bn_rows[:, :, 3, :],
                                        ALU.subtract).then_inc(bn_step, 1)
                pool.wait_ge(bn_step, 3)
                nc.gpsimd.tensor_tensor(bn_tmp[:, 1], bn_tmp[:, 0], exps, ALU.pow).then_inc(bn_step, 1)
                pool.wait_ge(bn_step, 4)
                scale = bn_out[:, 0:4:2, :]
                shift = bn_out[:, 1:4:2, :]
                nc.gpsimd.tensor_tensor(scale, bn_rows[:, :, 0, :], bn_tmp[:, 1], ALU.mult).then_inc(bn_step, 1)
                pool.wait_ge(bn_step, 5)
                nc.gpsimd.tensor_tensor(bn_tmp[:, 3], bn_tmp[:, 2], scale, ALU.mult).then_inc(bn_step, 1)
                pool.wait_ge(bn_step, 6)
                nc.gpsimd.tensor_tensor(shift, bn_tmp[:, 3], bn_rows[:, :, 2, :], ALU.add).then_inc(bn_rows_done, 1)

                def step(g):
                    nxt = ago(g, -1)
                    if exists(nxt):
                        rstd_1(nxt)
                    b = ago(g, 1)
                    if exists(b):
                        p = b[1]
                        pool.wait_ge(stats2_done, num(b) + 1)
                        wait(pool, nb2_done, num(b))
                        nc.gpsimd.tensor_tensor(ve2[:, :], mv2[p][:, :, 1], eps_cols[:, :], ALU.add)
                        nc.gpsimd.tensor_tensor(neg_mean2[:, :], mv2[p][:, :, 0], minus_one[:, :],
                                                ALU.mult).then_inc(ve2_done, 1)
                        pool.wait_ge(ve2_done, num(b) + 1)
                        nc.gpsimd.tensor_tensor(rstd2[p][:, :], ve2[:, :], minus_half[:, 0:GB],
                                                ALU.pow).then_inc(rstd2_done, 1)
                        pool.wait_ge(rstd2_done, num(b) + 1)
                        nc.gpsimd.tensor_tensor(nb2[p][:, :], neg_mean2[:, :], rstd2[p][:, :],
                                                ALU.mult).then_inc(nb2_done, 1)
                    t = ago(g, 2)
                    if exists(t):
                        pool.wait_ge(xn2_done, num(t) + 1)
                        wait(pool, acc_done, num(t))
                        nc.gpsimd.tensor_tensor(acc[:, :, :], acc[:, :, :], xn2[t[1]][:, :, :],
                                                ALU.add).then_inc(acc_done, 1)

                over_groups(pool, step)

            @block.scalar
            def _(act):
                act.wait_ge(setup_T, 1)
                nc.scalar.activation(gwT[:, :, :], ps_h[:, 0:C, :], ACT.Copy).then_inc(setup_copied, 1)
                nc.scalar.activation(a_cols[:, :], ps_s[:, 0, 0:2 * C], ACT.Copy).then_inc(setup_copied, 1)
                act.wait_ge(setup_T, 2)
                nc.scalar.activation(va[:, :, :], ps_s[:, 1, 0:2 * C].rearrange("p (c k) -> p c k", k=2),
                                     ACT.Copy).then_inc(setup_copied, 1)
                act.wait_ge(setup_T, 3)
                nc.scalar.activation(bn_cols[:, :, :], ps_pT[:, 0, 0:4 * EC].rearrange("p (r k) -> p r k", r=4),
                                     ACT.Copy).then_inc(setup_copied, 1)

                for i in range(NW):
                    act.wait_ge(w_loaded[i % 4], 16 * (i // 4 + 1))
                    nc.scalar.activation(w_hi[:, i, :, :], w_stage[:, i % 4, :, :], ACT.Copy).then_inc(w_hi_done, 1)

                def step(g):
                    p = g[1]
                    b = ago(g, 1)
                    if exists(b):
                        act.wait_ge(pT_ready, num(b) + 1)
                        nc.scalar.activation(pT[:, :, :], ps_pT[:, :, :], ACT.Copy).then_inc(pT_copied, 1)
                    if exists(g):
                        act.wait_ge(xT_ready, num(g) + 1)
                        wait(act, wh_ready, num(g))
                        nc.scalar.activation(xnT[:, :, :], ps_xT[:, :, :], ACT.Copy).then_inc(xT_copied, 1)
                    t = ago(g, 2)
                    if exists(t):
                        act.wait_ge(nb2_done, num(t) + 1)
                        wait(act, acc_done, num(t) - 1)
                        for b4 in range(GB):
                            last = nc.scalar.activation(xn2[t[1]][:, b4, :], x1[t[1]][:, b4, :], ACT.Identity,
                                                        bias=nb2[t[1]][:, b4:b4 + 1], scale=rstd2[t[1]][:, b4:b4 + 1])
                        last.then_inc(xn2_done, 1)
                    if exists(g):
                        act.wait_ge(bias_done, num(g) + 1)
                        wait(act, p_done, num(g) - 1)
                        for b4 in range(GB):
                            nc.scalar.activation(e_sb[p][:, 0, b4, :], ps_s[:, b4, :], ACT.Exp,
                                                 bias=exp_bias[p][:, 0, b4:b4 + 1])
                            last = nc.scalar.activation(e_sb[p][:, 1, b4, :], ps_s[:, b4, :], ACT.Exp,
                                                        bias=exp_bias[p][:, 1, b4:b4 + 1], scale=SLOPE)
                        last.then_inc(e_done, 1)
                        act.wait_ge(wh_ready, num(g) + 1)
                        wait(act, h_ready, num(g) - 1)
                        nc.scalar.activation(wh[p][:, :, :], ps_wh[:, :, :], ACT.Copy).then_inc(wh_copied, 1)

                over_groups(act, step)

            @block.vector
            def _(dve):
                def stats_1(g):
                    dve.wait_ge(x_loaded[g[1]], 16 * (g[0] + 1))
                    for b4 in range(GB):
                        last = nc.vector.bn_stats(st1[:, b4, :], x_sb[g[1]][:, b4, :])
                    last.then_inc(bnst1, 1)

                def stats_1_waits(g):
                    dve.wait_ge(bnst1, num(g) + 1)
                    wait(dve, rstd1_done, num(g) - 1)

                def aggregate_1(g):
                    for b4 in range(GB):
                        last = nc.vector.bn_aggr(mv1[g[1]][:, b4, :], st1[:, b4, :])
                    last.then_inc(stats1_done, 1)

                stats_1((0, 0))
                stats_1_waits((0, 0))
                aggregate_1((0, 0))
                for i in range(NW):
                    dve.wait_ge(w_hi_done, i + 1)
                    nc.vector.tensor_tensor(w_lo[:, i, :, :], w_stage[:, i % 4, :, :],
                                            w_hi[:, i, :, :].bitcast(F32), ALU.subtract).then_inc(w_lo_done, 1)

                def step(g):
                    p = g[1]
                    b = ago(g, 1)
                    q = b[1]
                    if exists(b):
                        dve.wait_ge(e_done, num(b) + 1)
                        nc.vector.tensor_tensor(e_max[:, :, :], e_sb[q][:, 0, :, :], e_sb[q][:, 1, :, :],
                                                ALU.max).then_inc(e_max_done, 1)
                        dve.wait_ge(e_max_done, num(b) + 1)
                        dve.wait_ge(adj_loaded[q], 16 * (b[0] + 1))
                        wait(dve, pT_ready, num(b))
                        nc.vector.scalar_tensor_tensor(out=p_sb[:, :, :], in0=adj_sb[q][:, :, :], scalar=ADJ_EPS,
                                                       in1=e_max[:, :, :], op0=ALU.add,
                                                       op1=ALU.mult).then_inc(p_done, 1)
                    if exists(g):
                        dve.wait_ge(rstd1_done, num(g) + 1)
                        dve.wait_ge(stats1_done, num(g) + 1)
                        wait(dve, xT_ready, num(g))
                        for b4 in range(GB):
                            last = nc.vector.tensor_scalar(xn[:, b4, :], x_sb[p][:, b4, :], mv1[p][:, b4, 0:1],
                                                           rstd1[p][:, b4:b4 + 1], ALU.subtract, ALU.mult)
                        last.then_inc(xn_done, 1)
                    nxt = ago(g, -1)
                    if exists(nxt):
                        stats_1(nxt)
                    if exists(b):
                        dve.wait_ge(h_ready, num(b) + 1)
                        nc.vector.reciprocal(rinv[:, :], ps_rowsum).then_inc(rinv_done, 1)
                        dve.wait_ge(rinv_done, num(b) + 1)
                        dve.wait_ge(res_loaded[q], 16 * (b[0] + 1))
                        wait(dve, x1_stored[q], 16 * b[0])
                        wait(dve, xn2_done, num(b) - 1)
                        for b4 in range(GB):
                            last = nc.vector.scalar_tensor_tensor(out=x1[q][:, b4, :], in0=ps_h[:, b4, :],
                                                                  scalar=rinv[:, b4:b4 + 1], in1=res[q][:, b4, :],
                                                                  op0=ALU.mult, op1=ALU.add)
                        last.then_inc(x1_done, 1)
                    if exists(g):
                        if exists(nxt):
                            stats_1_waits(nxt)
                        dve.wait_ge(s_ready, num(g) + 1)
                        nc.vector.tensor_copy(s_sb[p][:, :, :], ps_cols).then_inc(s_copied, 1)
                        if exists(nxt):
                            aggregate_1(nxt)
                    if exists(b):
                        dve.wait_ge(x1_done, num(b) + 1)
                        for b4 in range(GB):
                            last = nc.vector.bn_stats(st2[:, b4, :], x1[q][:, b4, :])
                        last.then_inc(bnst2, 1)
                        dve.wait_ge(bnst2, num(b) + 1)
                        wait(dve, nb2_done, num(b) - 1)
                    if exists(g):
                        dve.wait_ge(s2b_ready, num(g) + 1)
                        nc.vector.tensor_reduce(s2max[:, :], ps_s[:, :, :], AX_X, ALU.max).then_inc(s2max_done, 1)
                    if exists(b):
                        for b4 in range(GB):
                            last = nc.vector.bn_aggr(mv2[q][:, b4, :], st2[:, b4, :])
                        last.then_inc(stats2_done, 1)
                    if exists(g):
                        dve.wait_ge(s2max_done, num(g) + 1)
                        dve.wait_ge(s_copied, num(g) + 1)
                        nc.vector.scalar_tensor_tensor(out=neg_u[:, :], in0=s2max[:, :], scalar=-1.0,
                                                       in1=s_sb[p][:, :, 0], op0=ALU.mult,
                                                       op1=ALU.subtract).then_inc(neg_u_done, 1)
                        dve.wait_ge(neg_u_done, num(g) + 1)
                        nc.vector.scalar_tensor_tensor(out=neg_m[:, :], in0=neg_u[:, :], scalar=SLOPE,
                                                       in1=neg_u[:, :], op0=ALU.mult,
                                                       op1=ALU.min).then_inc(neg_m_done, 1)
                        dve.wait_ge(neg_m_done, num(g) + 1)
                        wait(dve, e_done, num(g) - 1)
                        nc.vector.tensor_tensor(exp_bias[p][:, 0, :], s_sb[p][:, :, 0], neg_m[:, :], ALU.add)
                        nc.vector.scalar_tensor_tensor(out=exp_bias[p][:, 1, :], in0=s_sb[p][:, :, 0], scalar=SLOPE,
                                                       in1=neg_m[:, :], op0=ALU.mult,
                                                       op1=ALU.add).then_inc(bias_done, 1)

                over_groups(dve, step)

            @block.tensor
            def _(pe):
                pe.wait_ge(setup_done, 1)
                pe.wait_ge(small_loaded, 16 * N_SMALL)
                for m in range(C):
                    for c in range(C):
                        nc.tensor.transpose(ps_h[:, m, c * P:(c + 1) * P], gw[:, c, m * P:(m + 1) * P], ident[:, :])
                nc.tensor.transpose(ps_s[:, 0, 0:2 * C], a_rows[:, :], ident[0:2 * C, 0:2 * C]).then_inc(setup_T, 1)
                pe.wait_ge(setup_copied, 2)
                a_pair = a_cols[:, :].rearrange("p (k m) -> p m k", k=2)
                for c in range(C):
                    for m in range(C):
                        last = nc.tensor.matmul(ps_s[:, 1, 2 * c:2 * c + 2], gwT[:, m, c * P:(c + 1) * P],
                                                a_pair[:, m, :], start=(m == 0), stop=(m == C - 1))
                last.then_inc(setup_T, 1)
                pe.wait_ge(bn_rows_done, 1)
                for r in range(4):
                    last = nc.tensor.transpose(ps_pT[:, 0, r * EC:(r + 1) * EC], bn_out[:, r, :], ident[0:EC, 0:EC])
                last.then_inc(setup_T, 1)
                pe.wait_ge(setup_copied, 4)

                def step(g):
                    p = g[1]
                    b = ago(g, 1)
                    q = b[1]
                    if exists(b):
                        pe.wait_ge(p_done, num(b) + 1)
                        wait(pe, rinv_done, num(b))
                        for b4 in range(GB):
                            last = nc.tensor.transpose(ps_pT[:, b4, :], p_sb[:, b4, :], ident[:, :])
                        last.then_inc(pT_ready, 1)
                    if exists(g):
                        pe.wait_ge(xn_done, num(g) + 1)
                        wait(pe, xT_copied, num(g))
                        for c in range(C):
                            for b4 in range(GB):
                                last = nc.tensor.transpose(ps_xT[:, c, b4 * N:(b4 + 1) * N],
                                                           xn[:, b4, c * P:(c + 1) * P], ident[:, :])
                        last.then_inc(xT_ready, 1)
                    if exists(b):
                        pe.wait_ge(pT_copied, num(b) + 1)
                        pe.wait_ge(wh_copied, num(b) + 1)
                        wait(pe, x1_done, num(b))
                        for b4 in range(GB):
                            nc.tensor.matmul(ps_h[:, b4, :], pT[:, b4, :], wh[q][:, b4, :], start=True, stop=True)
                            last = nc.tensor.matmul(ps_rowsum[:, b4:b4 + 1], pT[:, b4, :], ones_col[:, :],
                                                    start=True, stop=True)
                        last.then_inc(h_ready, 1)
                    if exists(g):
                        pe.wait_ge(xT_copied, num(g) + 1)
                        wait(pe, e_done, num(g))
                        wait(pe, s2max_done, num(g))
                        for b4 in range(GB):
                            for c in range(C):
                                last = nc.tensor.matmul(ps_cols[:, b4, :], xnT[:, c, b4 * N:(b4 + 1) * N],
                                                        va[:, c, :], start=(c == 0), stop=(c == C - 1))
                        last.then_inc(s_ready, 1)
                        wait(pe, wh_copied, num(g))

                        def project(graphs):
                            for b4 in graphs:
                                for c in range(C):
                                    mm = nc.tensor.matmul(ps_wh[:, b4, :], xnT[:, c, b4 * N:(b4 + 1) * N],
                                                          gw[:, c, :], start=(c == 0), stop=(c == C - 1))
                            return mm

                        project(range(GB // 2))
                        pe.wait_ge(s_copied, num(g) + 1)
                        for b4 in range(GB):
                            last = nc.tensor.matmul(ps_s[:, b4, :], s_sb[p][:, b4, 1:2].to_broadcast([P, P]),
                                                    ident[:, :], start=True, stop=True)
                        last.then_inc(s2b_ready, 1)
                        project(range(GB // 2, GB)).then_inc(wh_ready, 1)

                over_groups(pe, step)

        with ExitStack() as sbk:
            def sbb(name, shape, dt=F32):
                return sb(name, shape, dt, sbk)

            def psb(name, shape):
                return sbk.enter_context(nc.psum_tensor(name, shape, F32))

            feat = sbb("feat", [P, D])
            featT = sbb("featT", [P, C, P])
            logits = sbb("logits", [P, E])
            neg_max = sbb("neg_max", [P, 1])
            e_w = sbb("e_w", [P, E])
            e_sum = sbb("e_sum", [P, 1])
            e_rinv = sbb("e_rinv", [P, 1])
            w_node = sbb("w_node", [P, E])
            w_nodeT = sbb("w_nodeT", [E, P])
            w_bc = sbb("w_bc", [P, E, P])
            bias_out = sbb("bias_out", [P, D])
            x1t = sbb("x1t", [P, GB, D])
            st = sbb("st", [P, GB, 6])
            mv = sbb("mv", [P, GB, 2])
            ve = sbb("ve", [P, GB])
            rstd = sbb("rstd", [P, GB])
            xnb = sbb("xnb", [P, GB, D])
            xT_hi = sbb("xT_hi", [P, C, T], F32R)
            xT_lo = sbb("xT_lo", [P, C, T], F32R)
            h1 = sbb("h1", [P, C, T])
            h1_hi = [sbb(f"h1_hi{i}", [P, C, T], F32R) for i in range(2)]
            h1_lo = [sbb(f"h1_lo{i}", [P, C, T], F32R) for i in range(2)]
            h2 = sbb("h2", [P, C, T])
            h2w = sbb("h2w", [P, C, T])
            h2_hi = [sbb(f"h2_hi{i}", [P, C, T], F32R) for i in range(2)]
            h2_lo = [sbb(f"h2_lo{i}", [P, C, T], F32R) for i in range(2)]
            yT = sbb("yT", [P, C, T])
            resb = sbb("resb", [P, GB, D])
            out_sb = sbb("out_sb", [P, GB, D])

            ps_l1 = psb("ps_l1", [P, C, T])
            ps_l2 = psb("ps_l2", [P, C, T])
            ps_y = psb("ps_y", [P, C, T])
            ps_t = psb("ps_t", [P, GB * D])
            ps_t_x = ps_t[:, :].rearrange("p (c n) -> p c n", c=C)
            ps_t_y = ps_t[:, :].rearrange("p (b d) -> p b d", b=GB)

            def semb(name):
                return sem(name, sbk)

            router = semb("router")
            router_pe = semb("router_pe")
            router_act = semb("router_act")
            x1_loaded = semb("x1_loaded")
            bnst = semb("bnst")
            stats_done = semb("stats_done")
            ve_done = semb("ve_done")
            rstd_done = semb("rstd_done")
            xnb_done = semb("xnb_done")
            xT_ready = semb("xTb_ready")
            xhi_done = semb("xhi_done")
            xlo_done = semb("xlo_done")
            l1_done = semb("l1_done")
            r1_done = semb("r1_done")
            hi1_done = semb("hi1_done")
            lo1_done = semb("lo1_done")
            l2_done = semb("l2_done")
            r2_done = semb("r2_done")
            m2_done = semb("m2_done")
            hi2_done = semb("hi2_done")
            lo2_done = semb("lo2_done")
            l3_done = semb("l3_done")
            y_copied = semb("y_copied")
            yT_ready = semb("yT_ready")
            res_loaded_b = semb("res_loaded_b")
            resb_done = semb("resb_done")
            out_done = semb("out_done")
            out_stored = semb("out_stored")

            def unit(t, e):
                return (t + e // E, e % E)

            def uno(u):
                return E * u[0] + u[1]

            def over_tiles(eng, first, body):
                first()
                body(0, False)
                with eng.Fori(1, G - 1) as t:
                    body(t, False)
                body(G - 1, True)

            def steps(t, last):
                for s in range(1, E + 1):
                    us = [unit(t, s + 2), unit(t, s + 1), unit(t, s)]
                    if last:
                        us = [u if isinstance(u[0], int) and u[0] < G else None for u in us]
                    yield (*us, s)

            block = sbk.enter_context(nc.Block())

            @block.sync
            def _(sp):
                def load_x1(t):
                    wait(sp, xnb_done, t)
                    sp.dma_start(x1t[:, :, :].rearrange("p b d -> p (b d)"), x1_dram[t]).then_inc(x1_loaded, 16)

                def first():
                    load_x1(0)

                def body(t, last):
                    if not last:
                        load_x1(t + 1)
                    wait(sp, out_done, t)
                    sp.dma_start(resb[:, :, :].rearrange("p b d -> p (b d)"), x1_dram[t]).then_inc(res_loaded_b, 16)
                    sp.wait_ge(out_done, t + 1)
                    sp.dma_start(out_g[t], out_sb[:, :, :]).then_inc(out_stored, 16)

                over_tiles(sp, first, body)
                sp.wait_ge(out_stored, 16 * G)

            @block.gpsimd
            def _(pool):
                def norm(t):
                    pool.wait_ge(stats_done, t + 1)
                    nc.gpsimd.tensor_tensor(ve[:, :], mv[:, :, 1], eps_cols[:, :], ALU.add).then_inc(ve_done, 1)
                    pool.wait_ge(ve_done, t + 1)
                    nc.gpsimd.tensor_tensor(rstd[:, :], ve[:, :], minus_half[:, 0:GB], ALU.pow).then_inc(rstd_done, 1)

                def first():
                    norm(0)
                    pool.wait_ge(router_act, 6)

                def body(t, last):
                    if not last:
                        norm(t + 1)
                    pool.wait_ge(res_loaded_b, 16 * (t + 1))
                    nc.gpsimd.tensor_tensor(resb[:, :, :], resb[:, :, :],
                                            bias_out[:, None, :].to_broadcast([P, GB, D]),
                                            ALU.add).then_inc(resb_done, 1)

                over_tiles(pool, first, body)

            @block.scalar
            def _(act):
                def relu(u, psum, ready, h, done, row):
                    e = u[1]
                    for c in range(C):
                        act.wait_ge(ready, 2 * uno(u) + c + 1)
                        last = nc.scalar.activation(h[:, c, :], psum[:, c, :], ACT.Relu,
                                                    bias=bn_cols[:, row + 1, C * e + c:C * e + c + 1],
                                                    scale=bn_cols[:, row, C * e + c:C * e + c + 1])
                    last.then_inc(done, 1)

                def layer_1(u):
                    wait(act, lo1_done, uno(u))
                    relu(u, ps_l1, l1_done, h1, r1_done, 0)
                    act.wait_ge(r1_done, uno(u) + 1)
                    wait(act, l2_done, 2 * (uno(u) - 1))
                    nc.scalar.activation(h1_hi[u[1] % 2][:, :, :], h1[:, :, :], ACT.Copy).then_inc(hi1_done, 1)

                def layer_2(u):
                    wait(act, m2_done, uno(u))
                    relu(u, ps_l2, l2_done, h2, r2_done, 2)
                    act.wait_ge(m2_done, uno(u) + 1)
                    wait(act, l3_done, uno(u) - 1)
                    nc.scalar.activation(h2_hi[u[1] % 2][:, :, :], h2w[:, :, :], ACT.Copy).then_inc(hi2_done, 1)

                def x_high(t):
                    act.wait_ge(xT_ready, t + 1)
                    wait(act, l1_done, 2 * E * t)
                    nc.scalar.activation(xT_hi[:, :, :], ps_t_x, ACT.Copy).then_inc(xhi_done, 1)

                def y_copy(t):
                    act.wait_ge(l3_done, E * (t + 1))
                    wait(act, yT_ready, t)
                    nc.scalar.activation(yT[:, :, :], ps_y[:, :, :], ACT.Copy).then_inc(y_copied, 1)

                def first():
                    act.wait_ge(router_pe, 1)
                    nc.scalar.activation(featT[:, :, :], ps_l1[:, 0, 0:D].rearrange("p (c n) -> p c n", c=C),
                                         ACT.Copy, scale=1.0 / B).then_inc(router_act, 1)
                    act.wait_ge(router, 4)
                    nc.scalar.activation(e_w[:, :], logits[:, :], ACT.Exp, bias=neg_max[:, :]).then_inc(router_act, 1)
                    act.wait_ge(router_pe, 3)
                    nc.scalar.activation(w_bc[:, :, :], ps_l2[:, :, :].rearrange("p c (e n) -> p (c e) n", n=P),
                                         ACT.Copy).then_inc(router_act, 1)
                    nc.scalar.activation(w_nodeT[:, :], ps_y[0:E, 0, 0:P], ACT.Copy).then_inc(router_act, 1)
                    act.wait_ge(router_pe, 4)
                    nc.scalar.activation(bias_out[:, :], ps_y[:, 1, 0:D], ACT.Copy).then_inc(router_act, 2)
                    x_high(0)
                    layer_1((0, 0))
                    layer_1((0, 1))
                    layer_2((0, 0))
                    layer_1((0, 2))
                    layer_2((0, 1))

                def body(t, last):
                    for u1, u2, u3, s in steps(t, last):
                        if s == 5 + 1 and not last:
                            x_high(t + 1)
                        if s == E:
                            y_copy(t)
                        if u1:
                            layer_1(u1)
                        if u2:
                            layer_2(u2)

                over_tiles(act, first, body)

            @block.vector
            def _(dve):
                def norm(t):
                    dve.wait_ge(x1_loaded, 16 * (t + 1))
                    for b4 in range(GB):
                        last = nc.vector.bn_stats(st[:, b4, :], x1t[:, b4, :])
                    last.then_inc(bnst, 1)

                def aggregate(t):
                    for b4 in range(GB):
                        last = nc.vector.bn_aggr(mv[:, b4, :], st[:, b4, :])
                    last.then_inc(stats_done, 1)

                def normalise(t):
                    dve.wait_ge(rstd_done, t + 1)
                    dve.wait_ge(stats_done, t + 1)
                    for b4 in range(GB):
                        last = nc.vector.tensor_scalar(xnb[:, b4, :], x1t[:, b4, :], mv[:, b4, 0:1],
                                                       rstd[:, b4:b4 + 1], ALU.subtract, ALU.mult)
                    last.then_inc(xnb_done, 1)

                def x_low(t):
                    dve.wait_ge(xhi_done, t + 1)
                    nc.vector.tensor_tensor(xT_lo[:, :, :], ps_t_x, xT_hi[:, :, :].bitcast(F32),
                                            ALU.subtract).then_inc(xlo_done, 1)

                def layer_1(u):
                    dve.wait_ge(hi1_done, uno(u) + 1)
                    p = u[1] % 2
                    nc.vector.tensor_tensor(h1_lo[p][:, :, :], h1[:, :, :], h1_hi[p][:, :, :].bitcast(F32),
                                            ALU.subtract).then_inc(lo1_done, 1)

                def layer_2(u):
                    e, p = u[1], u[1] % 2
                    dve.wait_ge(r2_done, uno(u) + 1)
                    wait(dve, lo2_done, uno(u))
                    nc.vector.tensor_tensor(h2w[:, :, :].rearrange("p c (b n) -> p (c b) n", n=N),
                                            h2[:, :, :].rearrange("p c (b n) -> p (c b) n", n=N),
                                            w_bc[:, e:e + 1, :].to_broadcast([P, C * GB, N]),
                                            ALU.mult).then_inc(m2_done, 1)
                    dve.wait_ge(hi2_done, uno(u) + 1)
                    nc.vector.tensor_tensor(h2_lo[p][:, :, :], h2w[:, :, :], h2_hi[p][:, :, :].bitcast(F32),
                                            ALU.subtract).then_inc(lo2_done, 1)

                def out_add(t):
                    dve.wait_ge(yT_ready, t + 1)
                    dve.wait_ge(resb_done, t + 1)
                    wait(dve, out_stored, 16 * t)
                    nc.vector.tensor_tensor(out_sb[:, :, :], ps_t_y, resb[:, :, :], ALU.add).then_inc(out_done, 1)

                def first():
                    norm(0)
                    dve.wait_ge(bnst, 1)
                    aggregate(0)
                    nc.vector.tensor_reduce(feat[:, :], acc[:, :, :].rearrange("p b d -> p d b"), AX_X,
                                            ALU.add).then_inc(router, 1)
                    normalise(0)
                    dve.wait_ge(router_pe, 2)
                    nc.vector.tensor_tensor(logits[:, :], ps_l1[:, 1, 0:E], br_sb[:, :], ALU.add).then_inc(router, 1)
                    dve.wait_ge(router, 2)
                    nc.vector.tensor_reduce(neg_max[:, :], logits[:, :], AX_X, ALU.max, negate=True).then_inc(router, 2)
                    dve.wait_ge(router_act, 2)
                    nc.vector.reduce_sum(e_sum[:, :], e_w[:, :], AX_X).then_inc(router, 1)
                    dve.wait_ge(router, 5)
                    nc.vector.reciprocal(e_rinv[:, :], e_sum[:, :]).then_inc(router, 1)
                    dve.wait_ge(router, 6)
                    nc.vector.tensor_scalar(w_node[:, :], e_w[:, :], e_rinv[:, :], None, ALU.mult).then_inc(router, 1)
                    dve.wait_ge(router_act, 4)
                    x_low(0)
                    layer_1((0, 0))
                    layer_1((0, 1))
                    layer_2((0, 0))
                    layer_1((0, 2))
                    layer_2((0, 1))

                def body(t, last):
                    for u1, u2, u3, s in steps(t, last):
                        if s == 2 and not last:
                            norm(t + 1)
                            dve.wait_ge(bnst, t + 2)
                        if s == 3 and not last:
                            normalise(t + 1)
                        if s == 5 + 1 and not last:
                            x_low(t + 1)
                        if u1:
                            layer_1(u1)
                        if s == 2 and not last:
                            aggregate(t + 1)
                        if u2:
                            layer_2(u2)
                    out_add(t)

                over_tiles(dve, first, body)

            @block.tensor
            def _(pe):
                def product(acc_ps, i, src_hi, src_lo, m, start, stop):
                    cols = slice(m * P, (m + 1) * P)
                    terms = [(w, s, c) for c in range(C) for w, s in ((w_hi, src_hi), (w_hi, src_lo), (w_lo, src_hi))]
                    for n, (w, s, c) in enumerate(terms):
                        mm = nc.tensor.matmul(acc_ps, w[:, i, c, cols], s[:, c, :], start=start and n == 0,
                                              stop=stop and n == len(terms) - 1)
                    return mm

                def layer_1(u):
                    t, e = u
                    if e == 0:
                        pe.wait_ge(xlo_done, t + 1)
                    wait(pe, r1_done, uno(u))
                    for m in range(C):
                        product(ps_l1[:, m, :], e, xT_hi, xT_lo, m, True, True).then_inc(l1_done, 1)

                def layer_2(u):
                    e = u[1]
                    pe.wait_ge(lo1_done, uno(u) + 1)
                    wait(pe, r2_done, uno(u))
                    for m in range(C):
                        product(ps_l2[:, m, :], E + e, h1_hi[e % 2], h1_lo[e % 2], m, True, True).then_inc(l2_done, 1)

                def layer_3(u):
                    t, e = u
                    pe.wait_ge(lo2_done, uno(u) + 1)
                    if e == 0:
                        wait(pe, y_copied, t)
                    for m in range(C):
                        mm = product(ps_y[:, m, :], 2 * E + e, h2_hi[e % 2], h2_lo[e % 2], m, e == 0, e == E - 1)
                    mm.then_inc(l3_done, 1)

                def x_transpose(t):
                    pe.wait_ge(xnb_done, t + 1)
                    wait(pe, out_done, t - 1)
                    for c in range(C):
                        for b4 in range(GB):
                            last = nc.tensor.transpose(ps_t_x[:, c, b4 * N:(b4 + 1) * N],
                                                       xnb[:, b4, c * P:(c + 1) * P], ident[:, :])
                    last.then_inc(xT_ready, 1)

                def y_transpose(t):
                    pe.wait_ge(y_copied, t + 1)
                    pe.wait_ge(xlo_done, t + 2 if not (isinstance(t, int) and t == G - 1) else G)
                    for b4 in range(GB):
                        for m in range(C):
                            last = nc.tensor.transpose(ps_t_y[:, b4, m * P:(m + 1) * P],
                                                       yT[:, m, b4 * N:(b4 + 1) * N], ident[:, :])
                    last.then_inc(yT_ready, 1)

                def first():
                    pe.wait_ge(router, 1)
                    for c in range(C):
                        last = nc.tensor.transpose(ps_l1[:, 0, c * P:(c + 1) * P], feat[:, c * P:(c + 1) * P],
                                                   ident[:, :])
                    last.then_inc(router_pe, 1)
                    x_transpose(0)
                    pe.wait_ge(router_act, 1)
                    for c in range(C):
                        last = nc.tensor.matmul(ps_l1[:, 1, 0:E], featT[:, c, :], wr_sb[:, c, :],
                                                start=(c == 0), stop=(c == C - 1))
                    last.then_inc(router_pe, 1)
                    pe.wait_ge(router, 7)
                    w_out = ps_l2[:, :, :].rearrange("p c (e n) -> p (c e) n", n=P)
                    for e in range(E):
                        nc.tensor.matmul(w_out[:, e, :], w_node[:, e:e + 1].to_broadcast([P, P]), ident[:, :],
                                         start=True, stop=True)
                    nc.tensor.transpose(ps_y[0:E, 0, 0:P], w_node[:, :], ident[:, :]).then_inc(router_pe, 1)
                    pe.wait_ge(router_act, 4)
                    nc.tensor.matmul(ps_y[:, 1, 0:D], w_nodeT[:, :], bo_sb[:, :], start=True,
                                     stop=True).then_inc(router_pe, 1)
                    pe.wait_ge(router_act, 6)
                    layer_1((0, 0))
                    layer_1((0, 1))
                    layer_2((0, 0))
                    layer_1((0, 2))
                    layer_2((0, 1))
                    layer_3((0, 0))

                def body(t, last):
                    for u1, u2, u3, s in steps(t, last):
                        if u1:
                            layer_1(u1)
                        if s == 4 and not last:
                            x_transpose(t + 1)
                        if u2:
                            layer_2(u2)
                        if u3:
                            layer_3(u3)
                    y_transpose(t)

                over_tiles(pe, first, body)


_INS = ["x", "adj", "L0_gnn_W", "L0_gnn_a", "L0_ffn_Wr", "L0_ffn_br", "L0_ffn_W1", "L0_ffn_b1", "L0_ffn_g1",
        "L0_ffn_be1", "L0_ffn_m1", "L0_ffn_v1", "L0_ffn_W2", "L0_ffn_b2", "L0_ffn_g2", "L0_ffn_be2", "L0_ffn_m2",
        "L0_ffn_v2", "L0_ffn_Wo", "L0_ffn_bo"]


def kernel(**inputs):
    import numpy as _np
    import concourse.bacc as _bacc
    from concourse.bass_utils import run_bass_kernel_spmd as _run

    nc = _bacc.Bacc("TRN2", target_bir_lowering=False, num_devices=1)
    arrays, args = {}, []
    for name in _INS:
        a = _np.ascontiguousarray(inputs[name])
        arrays[f"in_{name}"] = a
        args.append(nc.dram_tensor(f"in_{name}", a.shape, mybir.dt.from_np(a.dtype), kind="ExternalInput").ap())
    out = nc.dram_tensor("out_0", inputs["x"].shape, F32, kind="ExternalOutput").ap()
    adj_ffn(nc, *args, out)
    r = _run(nc, [arrays], core_ids=[0])
    return r.results[0]["out_0"]
```

```python
from contextlib import ExitStack

import concourse.bass as bass
from concourse import mybir

F32 = mybir.dt.float32
F32R = mybir.dt.float32r
ALU = mybir.AluOpType
ACT = mybir.ActivationFunctionType
AX_X = mybir.AxisListType.X

P = 128
LN_EPS = 1e-5
ADJ_EPS = 1e-6
BN_EPS = 1e-3
SLOPE = 0.2


def wait(eng, sem, value):
    if isinstance(value, int) and value <= 0:
        return
    eng.wait_ge(sem, value)


def adj_ffn(nc, x, adj, gnn_w, gnn_a, wr, br, w1, b1, g1, be1, m1, v1, w2, b2, g2, be2, m2, v2, wo, bo, out):
    B, N, D = x.shape
    E = wr.shape[1]
    C = D // P
    GB = 4
    T = GB * N
    G = B // GB
    EC = E * C
    NW = 3 * E
    assert N == P and T == 512 and G % 2 == 0

    x_g = x.rearrange("(g b) n d -> g n b d", b=GB)
    adj_g = adj.rearrange("(g b) i j -> g i b j", b=GB)
    out_g = out.rearrange("(g b) n d -> g n b d", b=GB)
    x1_dram = nc.dram_tensor("x1_scratch", (G, P, GB * D), F32, kind="Internal").ap()

    with ExitStack() as ctx:
        def sb(name, shape, dt=F32, stack=ctx):
            return stack.enter_context(nc.sbuf_tensor(name, shape, dt))

        def sem(name, stack=ctx):
            return stack.enter_context(nc.semaphore(name))

        ident = sb("ident", [P, P])
        minus_half = sb("minus_half", [P, 2 * EC])
        eps_cols = sb("eps_cols", [P, GB])
        minus_one = sb("minus_one", [P, GB])
        w_hi = sb("w_hi", [P, NW, C, D], F32R)
        w_lo = sb("w_lo", [P, NW, C, D], F32R)
        bn_cols = sb("bn_cols", [P, 4, EC])
        acc = sb("acc", [P, GB, D])
        wr_sb = sb("wr_sb", [P, C, E])
        br_sb = sb("br_sb", [P, E])
        bo_sb = sb("bo_sb", [E, D])

        setup_done = sem("setup_done")
        phase_a_done = sem("phase_a_done")

        with ExitStack() as sa:
            def sba(name, shape, dt=F32):
                return sb(name, shape, dt, sa)

            def ps(name, shape):
                return sa.enter_context(nc.psum_tensor(name, shape, F32))

            w_stage = [sba(f"w_stage{i}", [P, C, D]) for i in range(2)]
            bn_rows = sba("bn_rows", [EC, 2, 5, P])
            bn_in = sba("bn_in", [P, 2, 5, EC])
            bn_tmp = sba("bn_tmp", [P, 4, 2, EC])
            a_rows = sba("a_rows", [2 * C, P])
            a_cols = sba("a_cols", [P, 2 * C])
            gw = sba("gw", [P, C, D])
            gwT = sba("gwT", [P, C, D])
            va = sba("va", [P, C, 2])
            x_sb = [sba(f"x_sb{i}", [P, GB, D]) for i in range(2)]
            res = [sba(f"res{i}", [P, GB, D]) for i in range(2)]
            adj_sb = [sba(f"adj_sb{i}", [P, GB, N]) for i in range(2)]
            st1 = sba("st1", [P, GB, 6])
            mv1 = [sba(f"mv1_{i}", [P, GB, 2]) for i in range(2)]
            ve1 = sba("ve1", [P, GB])
            neg_mean1 = sba("neg_mean1", [P, GB])
            nb1 = [sba(f"nb1_{i}", [P, GB]) for i in range(2)]
            rstd1 = [sba(f"rstd1_{i}", [P, GB]) for i in range(2)]
            xn = sba("xn", [P, GB, D])
            xnT = sba("xnT", [P, C, T])
            wh = [sba(f"wh{i}", [P, GB, D]) for i in range(2)]
            s_sb = [sba(f"s_sb{i}", [P, GB, 2]) for i in range(2)]
            s2max = sba("s2max", [P, GB])
            neg_u = sba("neg_u", [P, GB])
            neg_m = sba("neg_m", [P, GB])
            exp_bias = [sba(f"exp_bias{i}", [P, 2, GB]) for i in range(2)]
            e_sb = [sba(f"e_sb{i}", [P, 2, GB, N]) for i in range(2)]
            e_max = sba("e_max", [P, GB, N])
            p_sb = sba("p_sb", [P, GB, N])
            pT = sba("pT", [P, GB, N])
            rowsum = sba("rowsum", [P, GB])
            rinv = [sba(f"rinv{i}", [P, GB]) for i in range(2)]
            x1 = [sba(f"x1_{i}", [P, GB, D]) for i in range(2)]
            st2 = sba("st2", [P, GB, 6])
            mv2 = [sba(f"mv2_{i}", [P, GB, 2]) for i in range(2)]
            ve2 = sba("ve2", [P, GB])
            neg_mean2 = sba("neg_mean2", [P, GB])
            rstd2 = [sba(f"rstd2_{i}", [P, GB]) for i in range(2)]
            nb2 = [sba(f"nb2_{i}", [P, GB]) for i in range(2)]
            xn2 = [sba(f"xn2_{i}", [P, GB, D]) for i in range(2)]

            ps_xT = ps("ps_xT", [P, C, T])
            ps_wh = ps("ps_wh", [P, GB, D])
            ps_pT = ps("ps_pT", [P, GB, N])
            ps_h = ps("ps_h", [P, GB, D])
            ps_s = ps("ps_s", [P, GB, N])
            ps_cols = ps_s[:, 0, 0:2 * GB].rearrange("p (b k) -> p b k", k=2)
            ps_bn = ps_pT[:, :, :].rearrange("p b n -> p (b n)")[:, 0:10 * EC].rearrange("p (r k) -> p r k", k=EC)

            w_loaded = [sem(f"w_loaded{i}", sa) for i in range(2)]
            w_hi_done = sem("w_hi_done", sa)
            w_slots_free = sem("w_slots_free", sa)
            small_loaded = sem("small_loaded", sa)
            bn_step = sem("bn_step", sa)
            setup_T = sem("setup_T", sa)
            setup_copied = sem("setup_copied", sa)
            x_loaded = [sem(f"x_loaded{i}", sa) for i in range(2)]
            res_loaded = [sem(f"res_loaded{i}", sa) for i in range(2)]
            adj_loaded = [sem(f"adj_loaded{i}", sa) for i in range(2)]
            bnst1 = sem("bnst1", sa)
            stats1_done = sem("stats1_done", sa)
            ve1_done = sem("ve1_done", sa)
            rstd1_done = sem("rstd1_done", sa)
            nb1_done = sem("nb1_done", sa)
            xn_done = sem("xn_done", sa)
            xT_ready = sem("xT_ready", sa)
            xT_copied = sem("xT_copied", sa)
            wh_ready = sem("wh_ready", sa)
            wh_copied = sem("wh_copied", sa)
            s_ready = sem("s_ready", sa)
            s_copied = sem("s_copied", sa)
            s2b_ready = sem("s2b_ready", sa)
            s2max_done = sem("s2max_done", sa)
            neg_u_done = sem("neg_u_done", sa)
            neg_m_done = sem("neg_m_done", sa)
            bias_done = sem("bias_done", sa)
            e_max_done = sem("e_max_done", sa)
            e_done = sem("e_done", sa)
            p_done = sem("p_done", sa)
            pT_ready = sem("pT_ready", sa)
            pT_copied = sem("pT_copied", sa)
            h_ready = sem("h_ready", sa)
            rowsum_done = sem("rowsum_done", sa)
            rinv_done = sem("rinv_done", sa)
            x1_done = sem("x1_done", sa)
            x1_stored = [sem(f"x1_stored{i}", sa) for i in range(2)]
            bnst2 = sem("bnst2", sa)
            stats2_done = sem("stats2_done", sa)
            ve2_done = sem("ve2_done", sa)
            rstd2_done = sem("rstd2_done", sa)
            nb2_done = sem("nb2_done", sa)
            xn2_done = sem("xn2_done", sa)
            acc_done = sem("acc_done", sa)
            N_SMALL = 10 + 5
            K0, K1 = 3, G // 2 - 1
            assert 2 * (K1 - K0) == NW and E % 2 == 0

            w_dram = [w.rearrange("e (c p) n -> e p c n", p=P) for w in (w1, w2, wo)]

            def num(g):
                return 2 * g[0] + g[1]

            def ago(g, n):
                q = g[1] - n
                return (g[0] + q // 2, q % 2)

            def exists(g):
                return not isinstance(g[0], int) or 0 <= num(g) < G

            def over_groups(eng, step):
                for i in range(-2, 2 * K0):
                    step((i // 2, i % 2))
                with eng.Fori(K0, K1) as k:
                    step((k, 0))
                    step((k, 1))
                for i in range(2 * K1, G + 4):
                    step((i // 2, i % 2))

            def matrix(g):
                i = num(g) - 2 * K0
                return i if not isinstance(i, int) or 0 <= i < NW else None

            block = sa.enter_context(nc.Block())

            @block.sync
            def _(sp):
                def load_x(g):
                    p = g[1]
                    wait(sp, xn_done, num(g) - 1)
                    sp.dma_start(x_sb[p][:, :, :], x_g[num(g)]).then_inc(x_loaded[p], 16)

                load_x((0, 0))
                load_x((0, 1))
                sp.dma_start(gw[:, :, :], gnn_w.rearrange("(c p) n -> p c n", p=P)).then_inc(small_loaded, 16)
                sp.dma_start(a_rows[:, :], gnn_a.rearrange("(r p) o -> r (p o)", p=P)).then_inc(small_loaded, 16)
                sp.dma_start(wr_sb[:, :, :], wr.rearrange("(c p) e -> p c e", p=P)).then_inc(small_loaded, 16)
                sp.dma_start(br_sb[:, :], br.partition_broadcast(P)).then_inc(small_loaded, 16)
                sp.dma_start(bo_sb[:, :], bo).then_inc(small_loaded, 16)
                for layer, rows in enumerate(((g1, b1, be1, m1, v1), (g2, b2, be2, m2, v2))):
                    for i, r in enumerate(rows):
                        sp.dma_start(bn_rows[:, layer, i, :],
                                     r.rearrange("e (c p) -> (e c) p", p=P)).then_inc(small_loaded, 16)

                def step(g, layer=None):
                    p = g[1]
                    if exists(ago(g, -2)):
                        load_x(ago(g, -2))
                    if layer is not None:
                        i = matrix(g)
                        sp.wait_ge(w_slots_free, i + 1)
                        sp.dma_start(w_stage[p][:, :, :], w_dram[layer][i - layer * E]).then_inc(w_loaded[p], 16)
                    if exists(g):
                        wait(sp, p_done, num(g) - 1)
                        sp.dma_start(adj_sb[p][:, :, :], adj_g[num(g)]).then_inc(adj_loaded[p], 16)
                    r = ago(g, 1)
                    if exists(r):
                        wait(sp, x1_done, num(r) - 1)
                        sp.dma_start(res[r[1]][:, :, :], x_g[num(r)]).then_inc(res_loaded[r[1]], 16)
                    b = ago(g, 3)
                    if exists(b):
                        wait(sp, x1_done, num(b) + 1)
                        sp.dma_start(x1_dram[num(b)], x1[b[1]][:, :, :].rearrange("p b d -> p (b d)")
                                     ).then_inc(x1_stored[b[1]], 16)

                for i in range(2 * K0):
                    step((i // 2, i % 2))
                for layer in range(3):
                    with sp.Fori(K0 + layer * E // 2, K0 + (layer + 1) * E // 2) as k:
                        step((k, 0), layer)
                        step((k, 1), layer)
                for i in range(2 * K1, G + 4):
                    step((i // 2, i % 2))
                for p in range(2):
                    sp.wait_ge(x1_stored[p], 16 * (G // 2))

            @block.gpsimd
            def _(pool):
                nc.gpsimd.memset(ident[:, :], 0.0).then_inc(bn_step, 1)
                nc.gpsimd.memset(minus_half[:, :], -0.5).then_inc(w_slots_free, 2)
                nc.gpsimd.memset(eps_cols[:, :], LN_EPS)
                nc.gpsimd.memset(minus_one[:, :], -1.0)
                nc.gpsimd.memset(acc[:, :, :], 0.0)
                pool.wait_ge(bn_step, 1)
                nc.gpsimd.affine_select(out=ident[:, :], in_=ident[:, :], compare_op=ALU.not_equal, fill=1.0,
                                        base=0, pattern=[[-1, P]], channel_multiplier=1).then_inc(setup_done, 1)
                pool.wait_ge(setup_done, 1)

                def rstd_1(g):
                    p = g[1]
                    pool.wait_ge(stats1_done, num(g) + 1)
                    wait(pool, nb1_done, num(g))
                    nc.gpsimd.tensor_tensor(ve1[:, :], mv1[p][:, :, 1], eps_cols[:, :], ALU.add)
                    nc.gpsimd.tensor_tensor(neg_mean1[:, :], mv1[p][:, :, 0], minus_one[:, :],
                                            ALU.mult).then_inc(ve1_done, 1)
                    pool.wait_ge(ve1_done, num(g) + 1)
                    nc.gpsimd.tensor_tensor(rstd1[p][:, :], ve1[:, :], minus_half[:, 0:GB],
                                            ALU.pow).then_inc(rstd1_done, 1)
                    pool.wait_ge(rstd1_done, num(g) + 1)
                    nc.gpsimd.tensor_tensor(nb1[p][:, :], neg_mean1[:, :], rstd1[p][:, :],
                                            ALU.mult).then_inc(nb1_done, 1)

                pool.wait_ge(setup_copied, 4)
                exps = minus_half[:, :].rearrange("p (l n) -> p l n", l=2)
                scale = bn_cols[:, 0:4:2, :]
                shift = bn_cols[:, 1:4:2, :]
                nc.gpsimd.tensor_scalar(bn_tmp[:, 0], bn_in[:, :, 4, :], BN_EPS, None, ALU.add).then_inc(bn_step, 1)
                nc.gpsimd.tensor_tensor(bn_tmp[:, 2], bn_in[:, :, 1, :], bn_in[:, :, 3, :],
                                        ALU.subtract).then_inc(bn_step, 1)
                pool.wait_ge(bn_step, 3)
                nc.gpsimd.tensor_tensor(bn_tmp[:, 1], bn_tmp[:, 0], exps, ALU.pow).then_inc(bn_step, 1)
                pool.wait_ge(bn_step, 4)
                nc.gpsimd.tensor_tensor(scale, bn_in[:, :, 0, :], bn_tmp[:, 1], ALU.mult).then_inc(bn_step, 1)
                pool.wait_ge(bn_step, 5)
                nc.gpsimd.tensor_tensor(bn_tmp[:, 3], bn_tmp[:, 2], scale, ALU.mult).then_inc(bn_step, 1)
                pool.wait_ge(bn_step, 6)
                nc.gpsimd.tensor_tensor(shift, bn_tmp[:, 3], bn_in[:, :, 2, :], ALU.add)

                def step(g):
                    nxt = ago(g, -1)
                    if exists(nxt):
                        rstd_1(nxt)
                    t = ago(g, 4)
                    if exists(t):
                        p = t[1]
                        pool.wait_ge(stats2_done, num(t) + 1)
                        wait(pool, nb2_done, num(t))
                        nc.gpsimd.tensor_tensor(ve2[:, :], mv2[p][:, :, 1], eps_cols[:, :], ALU.add)
                        nc.gpsimd.tensor_tensor(neg_mean2[:, :], mv2[p][:, :, 0], minus_one[:, :],
                                                ALU.mult).then_inc(ve2_done, 1)
                        pool.wait_ge(ve2_done, num(t) + 1)
                        nc.gpsimd.tensor_tensor(rstd2[p][:, :], ve2[:, :], minus_half[:, 0:GB],
                                                ALU.pow).then_inc(rstd2_done, 1)
                        pool.wait_ge(rstd2_done, num(t) + 1)
                        nc.gpsimd.tensor_tensor(nb2[p][:, :], neg_mean2[:, :], rstd2[p][:, :],
                                                ALU.mult).then_inc(nb2_done, 1)
                        pool.wait_ge(xn2_done, num(t) + 1)
                        wait(pool, acc_done, num(t))
                        nc.gpsimd.tensor_tensor(acc[:, :, :], acc[:, :, :], xn2[t[1]][:, :, :],
                                                ALU.add).then_inc(acc_done, 1)
                    i = matrix(g)
                    if i is not None:
                        pool.wait_ge(w_hi_done, i + 1)
                        nc.gpsimd.tensor_tensor(w_lo[:, i, :, :], w_stage[g[1]][:, :, :],
                                                w_hi[:, i, :, :].bitcast(F32), ALU.subtract).then_inc(w_slots_free, 1)

                over_groups(pool, step)

            @block.scalar
            def _(act):
                act.wait_ge(setup_T, 1)
                nc.scalar.activation(gwT[:, :, :], ps_h[:, 0:C, :], ACT.Copy).then_inc(setup_copied, 1)
                nc.scalar.activation(a_cols[:, :], ps_s[:, 0, 0:2 * C], ACT.Copy).then_inc(setup_copied, 1)
                nc.scalar.activation(bn_in[:, :, :, :].rearrange("p l i k -> p (l i) k"), ps_bn,
                                     ACT.Copy).then_inc(setup_copied, 1)
                act.wait_ge(setup_T, 2)
                nc.scalar.activation(va[:, :, :], ps_s[:, 1, 0:2 * C].rearrange("p (c k) -> p c k", k=2),
                                     ACT.Copy).then_inc(setup_copied, 1)
                def normalise(g):
                    p = g[1]
                    act.wait_ge(nb1_done, num(g) + 1)
                    wait(act, xT_ready, num(g))
                    for b4 in range(GB):
                        last = nc.scalar.activation(xn[:, b4, :], x_sb[p][:, b4, :], ACT.Identity,
                                                    bias=nb1[p][:, b4:b4 + 1], scale=rstd1[p][:, b4:b4 + 1])
                    last.then_inc(xn_done, 1)


                def step(g):
                    p = g[1]
                    b = ago(g, 2)
                    if exists(b):
                        act.wait_ge(pT_ready, num(b) + 1)
                        wait(act, h_ready, num(b))
                        nc.scalar.activation(pT[:, :, :], ps_pT[:, :, :], ACT.Copy).then_inc(pT_copied, 1)
                    nxt = ago(g, -1)
                    if exists(nxt):
                        normalise(nxt)
                    t = ago(g, 4)
                    if exists(t):
                        act.wait_ge(nb2_done, num(t) + 1)
                        wait(act, acc_done, num(t) - 1)
                        for b4 in range(GB):
                            last = nc.scalar.activation(xn2[t[1]][:, b4, :], x1[t[1]][:, b4, :], ACT.Identity,
                                                        bias=nb2[t[1]][:, b4:b4 + 1], scale=rstd2[t[1]][:, b4:b4 + 1])
                        last.then_inc(xn2_done, 1)
                    if exists(g):
                        act.wait_ge(bias_done, num(g) + 1)
                        wait(act, p_done, num(g) - 1)
                        for b4 in range(GB):
                            nc.scalar.activation(e_sb[p][:, 0, b4, :], ps_s[:, b4, :], ACT.Exp,
                                                 bias=exp_bias[p][:, 0, b4:b4 + 1])
                            last = nc.scalar.activation(e_sb[p][:, 1, b4, :], ps_s[:, b4, :], ACT.Exp,
                                                        bias=exp_bias[p][:, 1, b4:b4 + 1], scale=SLOPE)
                        last.then_inc(e_done, 1)
                    if exists(nxt):
                        act.wait_ge(xT_ready, num(nxt) + 1)
                        wait(act, wh_ready, num(nxt))
                        nc.scalar.activation(xnT[:, :, :], ps_xT[:, :, :], ACT.Copy).then_inc(xT_copied, 1)
                    if exists(g):
                        act.wait_ge(wh_ready, num(g) + 1)
                        wait(act, h_ready, num(g) - 1)
                        nc.scalar.activation(wh[p][:, :, :], ps_wh[:, :, :], ACT.Copy).then_inc(wh_copied, 1)
                    i = matrix(g)
                    if i is not None:
                        act.wait_ge(w_loaded[p], 16 * (g[0] - K0 + 1))
                        nc.scalar.activation(w_hi[:, i, :, :], w_stage[p][:, :, :], ACT.Copy).then_inc(w_hi_done, 1)

                over_groups(act, step)

            @block.vector
            def _(dve):
                def stats_1(g):
                    wait(dve, stats1_done, num(g))
                    dve.wait_ge(x_loaded[g[1]], 16 * (g[0] + 1))
                    for b4 in range(GB):
                        last = nc.vector.bn_stats(st1[:, b4, :], x_sb[g[1]][:, b4, :])
                    last.then_inc(bnst1, 1)

                def aggregate_1(g):
                    for b4 in range(GB):
                        last = nc.vector.bn_aggr(mv1[g[1]][:, b4, :], st1[:, b4, :])
                    last.then_inc(stats1_done, 1)

                def aggregate_2(g):
                    for b4 in range(GB):
                        last = nc.vector.bn_aggr(mv2[g[1]][:, b4, :], st2[:, b4, :])
                    last.then_inc(stats2_done, 1)

                def step(g):
                    p = g[1]
                    b = ago(g, 3)
                    q = b[1]
                    if exists(b):
                        dve.wait_ge(h_ready, num(b) + 1)
                        dve.wait_ge(rinv_done, num(b) + 1)
                        dve.wait_ge(res_loaded[q], 16 * (b[0] + 1))
                        wait(dve, x1_stored[q], 16 * b[0])
                        wait(dve, xn2_done, num(b) - 1)
                        for b4 in range(GB):
                            last = nc.vector.scalar_tensor_tensor(out=x1[q][:, b4, :], in0=ps_h[:, b4, :],
                                                                  scalar=rinv[q][:, b4:b4 + 1], in1=res[q][:, b4, :],
                                                                  op0=ALU.mult, op1=ALU.add)
                        last.then_inc(x1_done, 1)
                    if exists(g):
                        dve.wait_ge(s_ready, num(g) + 1)
                        nc.vector.tensor_copy(s_sb[p][:, :, :], ps_cols).then_inc(s_copied, 1)
                    a = ago(g, 1)
                    r = a[1]
                    if exists(a):
                        dve.wait_ge(e_done, num(a) + 1)
                        nc.vector.tensor_tensor(e_max[:, :, :], e_sb[r][:, 0, :, :], e_sb[r][:, 1, :, :],
                                                ALU.max).then_inc(e_max_done, 1)
                        dve.wait_ge(e_max_done, num(a) + 1)
                        dve.wait_ge(adj_loaded[r], 16 * (a[0] + 1))
                        wait(dve, pT_ready, num(a))
                        nc.vector.scalar_tensor_tensor(out=p_sb[:, :, :], in0=adj_sb[r][:, :, :], scalar=ADJ_EPS,
                                                       in1=e_max[:, :, :], op0=ALU.add,
                                                       op1=ALU.mult).then_inc(p_done, 1)
                        dve.wait_ge(p_done, num(a) + 1)
                        nc.vector.tensor_reduce(rowsum[:, :], p_sb[:, :, :], AX_X, ALU.add).then_inc(rowsum_done, 1)
                    if exists(g):
                        dve.wait_ge(s2b_ready, num(g) + 1)
                        nc.vector.tensor_reduce(s2max[:, :], ps_s[:, :, :], AX_X, ALU.max).then_inc(s2max_done, 1)
                        dve.wait_ge(s2max_done, num(g) + 1)
                        dve.wait_ge(s_copied, num(g) + 1)
                        nc.vector.scalar_tensor_tensor(out=neg_u[:, :], in0=s2max[:, :], scalar=-1.0,
                                                       in1=s_sb[p][:, :, 0], op0=ALU.mult,
                                                       op1=ALU.subtract).then_inc(neg_u_done, 1)
                        dve.wait_ge(neg_u_done, num(g) + 1)
                        nc.vector.scalar_tensor_tensor(out=neg_m[:, :], in0=neg_u[:, :], scalar=SLOPE,
                                                       in1=neg_u[:, :], op0=ALU.mult,
                                                       op1=ALU.min).then_inc(neg_m_done, 1)
                        dve.wait_ge(neg_m_done, num(g) + 1)
                        wait(dve, e_done, num(g) - 1)
                        nc.vector.tensor_tensor(exp_bias[p][:, 0, :], s_sb[p][:, :, 0], neg_m[:, :], ALU.add)
                        nc.vector.scalar_tensor_tensor(out=exp_bias[p][:, 1, :], in0=s_sb[p][:, :, 0], scalar=SLOPE,
                                                       in1=neg_m[:, :], op0=ALU.mult,
                                                       op1=ALU.add).then_inc(bias_done, 1)
                    nxt = ago(g, -2)
                    if exists(nxt):
                        stats_1(nxt)
                    if exists(b):
                        wait(dve, stats2_done, num(b))
                        dve.wait_ge(x1_done, num(b) + 1)
                        for b4 in range(GB):
                            last = nc.vector.bn_stats(st2[:, b4, :], x1[q][:, b4, :])
                        last.then_inc(bnst2, 1)
                    if exists(nxt):
                        dve.wait_ge(bnst1, num(nxt) + 1)
                        wait(dve, nb1_done, num(nxt) - 1)
                    if exists(b):
                        dve.wait_ge(bnst2, num(b) + 1)
                        wait(dve, nb2_done, num(b) - 1)
                    if exists(a):
                        dve.wait_ge(rowsum_done, num(a) + 1)
                        nc.vector.reciprocal(rinv[r][:, :], rowsum[:, :]).then_inc(rinv_done, 1)
                    if exists(nxt):
                        aggregate_1(nxt)
                    if exists(b):
                        aggregate_2(b)

                over_groups(dve, step)

            @block.tensor
            def _(pe):
                pe.wait_ge(setup_done, 1)
                pe.wait_ge(small_loaded, 16 * N_SMALL)
                for m in range(C):
                    for c in range(C):
                        nc.tensor.transpose(ps_h[:, m, c * P:(c + 1) * P], gw[:, c, m * P:(m + 1) * P], ident[:, :])
                for r in range(10):
                    nc.tensor.transpose(ps_bn[:, r, :], bn_rows[:, r // 5, r % 5, :], ident[0:EC, 0:EC])
                nc.tensor.transpose(ps_s[:, 0, 0:2 * C], a_rows[:, :], ident[0:2 * C, 0:2 * C]).then_inc(setup_T, 1)
                pe.wait_ge(setup_copied, 2)
                a_pair = a_cols[:, :].rearrange("p (k m) -> p m k", k=2)
                for c in range(C):
                    for m in range(C):
                        last = nc.tensor.matmul(ps_s[:, 1, 2 * c:2 * c + 2], gwT[:, m, c * P:(c + 1) * P],
                                                a_pair[:, m, :], start=(m == 0), stop=(m == C - 1))
                last.then_inc(setup_T, 1)
                pe.wait_ge(setup_copied, 4)

                def step(g):
                    p = g[1]
                    b = ago(g, 2)
                    q = b[1]
                    if exists(b):
                        pe.wait_ge(p_done, num(b) + 1)
                        wait(pe, pT_copied, num(b))
                        for b4 in range(GB):
                            last = nc.tensor.transpose(ps_pT[:, b4, :], p_sb[:, b4, :], ident[:, :])
                        last.then_inc(pT_ready, 1)
                    if exists(g):
                        pe.wait_ge(xT_copied, num(g) + 1)
                        wait(pe, e_done, num(g))
                        wait(pe, s2max_done, num(g))
                        for b4 in range(GB):
                            for c in range(C):
                                last = nc.tensor.matmul(ps_cols[:, b4, :], xnT[:, c, b4 * N:(b4 + 1) * N],
                                                        va[:, c, :], start=(c == 0), stop=(c == C - 1))
                        last.then_inc(s_ready, 1)
                        wait(pe, wh_copied, num(g))

                        def project(graphs):
                            for b4 in graphs:
                                for c in range(C):
                                    mm = nc.tensor.matmul(ps_wh[:, b4, :], xnT[:, c, b4 * N:(b4 + 1) * N],
                                                          gw[:, c, :], start=(c == 0), stop=(c == C - 1))
                            return mm

                        project(range(GB // 2))
                        pe.wait_ge(s_copied, num(g) + 1)
                        for b4 in range(GB):
                            last = nc.tensor.matmul(ps_s[:, b4, :], s_sb[p][:, b4, 1:2].to_broadcast([P, P]),
                                                    ident[:, :], start=True, stop=True)
                        last.then_inc(s2b_ready, 1)
                        project(range(GB // 2, GB)).then_inc(wh_ready, 1)
                    nxt = ago(g, -1)
                    if exists(nxt):
                        pe.wait_ge(xn_done, num(nxt) + 1)
                        wait(pe, xT_copied, num(nxt))
                        for c in range(C):
                            for b4 in range(GB):
                                last = nc.tensor.transpose(ps_xT[:, c, b4 * N:(b4 + 1) * N],
                                                           xn[:, b4, c * P:(c + 1) * P], ident[:, :])
                        last.then_inc(xT_ready, 1)
                    if exists(b):
                        pe.wait_ge(pT_copied, num(b) + 1)
                        pe.wait_ge(wh_copied, num(b) + 1)
                        wait(pe, x1_done, num(b))
                        for b4 in range(GB):
                            last = nc.tensor.matmul(ps_h[:, b4, :], pT[:, b4, :], wh[q][:, b4, :], start=True,
                                                    stop=True)
                        last.then_inc(h_ready, 1)

                over_groups(pe, step)

        with ExitStack() as sbk:
            def sbb(name, shape, dt=F32):
                return sb(name, shape, dt, sbk)

            def psb(name, shape):
                return sbk.enter_context(nc.psum_tensor(name, shape, F32))

            feat = sbb("feat", [P, D])
            featT = sbb("featT", [P, C, P])
            logits = sbb("logits", [P, E])
            neg_max = sbb("neg_max", [P, 1])
            e_w = sbb("e_w", [P, E])
            e_sum = sbb("e_sum", [P, 1])
            e_rinv = sbb("e_rinv", [P, 1])
            w_node = sbb("w_node", [P, E])
            w_nodeT = sbb("w_nodeT", [E, P])
            w_bc = sbb("w_bc", [P, E, P])
            bias_out = sbb("bias_out", [P, D])
            x1t = sbb("x1t", [P, GB, D])
            st = sbb("st", [P, GB, 6])
            mv = sbb("mv", [P, GB, 2])
            ve = sbb("ve", [P, GB])
            rstd = sbb("rstd", [P, GB])
            xnb = sbb("xnb", [P, GB, D])
            xT_hi = sbb("xT_hi", [P, C, T], F32R)
            xT_lo = sbb("xT_lo", [P, C, T], F32R)
            h1 = sbb("h1", [P, C, T])
            h1_hi = [sbb(f"h1_hi{i}", [P, C, T], F32R) for i in range(2)]
            h1_lo = [sbb(f"h1_lo{i}", [P, C, T], F32R) for i in range(2)]
            h2 = sbb("h2", [P, C, T])
            h2w = sbb("h2w", [P, C, T])
            h2_hi = [sbb(f"h2_hi{i}", [P, C, T], F32R) for i in range(2)]
            h2_lo = [sbb(f"h2_lo{i}", [P, C, T], F32R) for i in range(2)]
            yT = sbb("yT", [P, C, T])
            resb = sbb("resb", [P, GB, D])
            out_sb = sbb("out_sb", [P, GB, D])

            ps_l1 = psb("ps_l1", [P, C, T])
            ps_l2 = psb("ps_l2", [P, C, T])
            ps_y = psb("ps_y", [P, C, T])
            ps_t = psb("ps_t", [P, GB * D])
            ps_t_x = ps_t[:, :].rearrange("p (c n) -> p c n", c=C)
            ps_t_y = ps_t[:, :].rearrange("p (b d) -> p b d", b=GB)

            def semb(name):
                return sem(name, sbk)

            router = semb("router")
            router_pe = semb("router_pe")
            router_act = semb("router_act")
            x1_loaded = semb("x1_loaded")
            bnst = semb("bnst")
            stats_done = semb("stats_done")
            ve_done = semb("ve_done")
            rstd_done = semb("rstd_done")
            xnb_done = semb("xnb_done")
            xT_ready = semb("xTb_ready")
            xhi_done = semb("xhi_done")
            xlo_done = semb("xlo_done")
            l1_done = semb("l1_done")
            r1_done = semb("r1_done")
            hi1_done = semb("hi1_done")
            lo1_done = semb("lo1_done")
            l2_done = semb("l2_done")
            r2_done = semb("r2_done")
            m2_done = semb("m2_done")
            hi2_done = semb("hi2_done")
            lo2_done = semb("lo2_done")
            l3_done = semb("l3_done")
            y_copied = semb("y_copied")
            yT_ready = semb("yT_ready")
            res_loaded_b = semb("res_loaded_b")
            resb_done = semb("resb_done")
            out_done = semb("out_done")
            out_stored = semb("out_stored")

            def unit(t, e):
                return (t + e // E, e % E)

            def uno(u):
                return E * u[0] + u[1]

            def over_tiles(eng, first, body):
                first()
                body(0, False)
                with eng.Fori(1, G - 1) as t:
                    body(t, False)
                body(G - 1, True)

            def steps(t, last):
                for s in range(1, E + 1):
                    us = [unit(t, s + 2), unit(t, s + 1), unit(t, s)]
                    if last:
                        us = [u if isinstance(u[0], int) and u[0] < G else None for u in us]
                    yield (*us, s)

            block = sbk.enter_context(nc.Block())

            @block.sync
            def _(sp):
                def load_x1(t):
                    wait(sp, xnb_done, t)
                    sp.dma_start(x1t[:, :, :].rearrange("p b d -> p (b d)"), x1_dram[t]).then_inc(x1_loaded, 16)

                def first():
                    load_x1(0)

                def body(t, last):
                    if not last:
                        load_x1(t + 1)
                    wait(sp, out_done, t)
                    sp.dma_start(resb[:, :, :].rearrange("p b d -> p (b d)"), x1_dram[t]).then_inc(res_loaded_b, 16)
                    sp.wait_ge(out_done, t + 1)
                    sp.dma_start(out_g[t], out_sb[:, :, :]).then_inc(out_stored, 16)

                over_tiles(sp, first, body)
                sp.wait_ge(out_stored, 16 * G)

            @block.gpsimd
            def _(pool):
                def norm(t):
                    pool.wait_ge(stats_done, t + 1)
                    nc.gpsimd.tensor_tensor(ve[:, :], mv[:, :, 1], eps_cols[:, :], ALU.add).then_inc(ve_done, 1)
                    pool.wait_ge(ve_done, t + 1)
                    nc.gpsimd.tensor_tensor(rstd[:, :], ve[:, :], minus_half[:, 0:GB], ALU.pow).then_inc(rstd_done, 1)

                def first():
                    norm(0)
                    pool.wait_ge(router_act, 6)

                def body(t, last):
                    if not last:
                        norm(t + 1)
                    pool.wait_ge(res_loaded_b, 16 * (t + 1))
                    nc.gpsimd.tensor_tensor(resb[:, :, :], resb[:, :, :],
                                            bias_out[:, None, :].to_broadcast([P, GB, D]),
                                            ALU.add).then_inc(resb_done, 1)

                over_tiles(pool, first, body)

            @block.scalar
            def _(act):
                def relu(u, psum, ready, h, done, row):
                    e = u[1]
                    for c in range(C):
                        act.wait_ge(ready, 2 * uno(u) + c + 1)
                        last = nc.scalar.activation(h[:, c, :], psum[:, c, :], ACT.Relu,
                                                    bias=bn_cols[:, row + 1, C * e + c:C * e + c + 1],
                                                    scale=bn_cols[:, row, C * e + c:C * e + c + 1])
                    last.then_inc(done, 1)

                def layer_1(u):
                    wait(act, lo1_done, uno(u))
                    relu(u, ps_l1, l1_done, h1, r1_done, 0)
                    act.wait_ge(r1_done, uno(u) + 1)
                    wait(act, l2_done, 2 * (uno(u) - 1))
                    nc.scalar.activation(h1_hi[u[1] % 2][:, :, :], h1[:, :, :], ACT.Copy).then_inc(hi1_done, 1)

                def layer_2(u):
                    wait(act, m2_done, uno(u))
                    relu(u, ps_l2, l2_done, h2, r2_done, 2)
                    act.wait_ge(m2_done, uno(u) + 1)
                    wait(act, l3_done, uno(u) - 1)
                    nc.scalar.activation(h2_hi[u[1] % 2][:, :, :], h2w[:, :, :], ACT.Copy).then_inc(hi2_done, 1)

                def x_high(t):
                    act.wait_ge(xT_ready, t + 1)
                    wait(act, l1_done, 2 * E * t)
                    nc.scalar.activation(xT_hi[:, :, :], ps_t_x, ACT.Copy).then_inc(xhi_done, 1)

                def y_copy(t):
                    act.wait_ge(l3_done, E * (t + 1))
                    wait(act, yT_ready, t)
                    nc.scalar.activation(yT[:, :, :], ps_y[:, :, :], ACT.Copy).then_inc(y_copied, 1)

                def first():
                    act.wait_ge(router_pe, 1)
                    nc.scalar.activation(featT[:, :, :], ps_l1[:, 0, 0:D].rearrange("p (c n) -> p c n", c=C),
                                         ACT.Copy, scale=1.0 / B).then_inc(router_act, 1)
                    act.wait_ge(router, 4)
                    nc.scalar.activation(e_w[:, :], logits[:, :], ACT.Exp, bias=neg_max[:, :]).then_inc(router_act, 1)
                    act.wait_ge(router_pe, 3)
                    nc.scalar.activation(w_bc[:, :, :], ps_l2[:, :, :].rearrange("p c (e n) -> p (c e) n", n=P),
                                         ACT.Copy).then_inc(router_act, 1)
                    nc.scalar.activation(w_nodeT[:, :], ps_y[0:E, 0, 0:P], ACT.Copy).then_inc(router_act, 1)
                    act.wait_ge(router_pe, 4)
                    nc.scalar.activation(bias_out[:, :], ps_y[:, 1, 0:D], ACT.Copy).then_inc(router_act, 2)
                    x_high(0)
                    layer_1((0, 0))
                    layer_1((0, 1))
                    layer_2((0, 0))
                    layer_1((0, 2))
                    layer_2((0, 1))

                def body(t, last):
                    for u1, u2, u3, s in steps(t, last):
                        if s == E:
                            y_copy(t)
                        if u1:
                            layer_1(u1)
                        if s == E - 3 and not last:
                            x_high(t + 1)
                        if u2:
                            layer_2(u2)

                over_tiles(act, first, body)

            @block.vector
            def _(dve):
                def norm(t):
                    dve.wait_ge(x1_loaded, 16 * (t + 1))
                    for b4 in range(GB):
                        last = nc.vector.bn_stats(st[:, b4, :], x1t[:, b4, :])
                    last.then_inc(bnst, 1)

                def aggregate(t):
                    for b4 in range(GB):
                        last = nc.vector.bn_aggr(mv[:, b4, :], st[:, b4, :])
                    last.then_inc(stats_done, 1)

                def normalise(t):
                    dve.wait_ge(rstd_done, t + 1)
                    dve.wait_ge(stats_done, t + 1)
                    for b4 in range(GB):
                        last = nc.vector.tensor_scalar(xnb[:, b4, :], x1t[:, b4, :], mv[:, b4, 0:1],
                                                       rstd[:, b4:b4 + 1], ALU.subtract, ALU.mult)
                    last.then_inc(xnb_done, 1)

                def x_low(t):
                    dve.wait_ge(xhi_done, t + 1)
                    nc.vector.tensor_tensor(xT_lo[:, :, :], ps_t_x, xT_hi[:, :, :].bitcast(F32),
                                            ALU.subtract).then_inc(xlo_done, 1)

                def layer_1(u):
                    dve.wait_ge(hi1_done, uno(u) + 1)
                    p = u[1] % 2
                    nc.vector.tensor_tensor(h1_lo[p][:, :, :], h1[:, :, :], h1_hi[p][:, :, :].bitcast(F32),
                                            ALU.subtract).then_inc(lo1_done, 1)

                def layer_2(u):
                    e, p = u[1], u[1] % 2
                    dve.wait_ge(r2_done, uno(u) + 1)
                    wait(dve, lo2_done, uno(u))
                    nc.vector.tensor_tensor(h2w[:, :, :].rearrange("p c (b n) -> p (c b) n", n=N),
                                            h2[:, :, :].rearrange("p c (b n) -> p (c b) n", n=N),
                                            w_bc[:, e:e + 1, :].to_broadcast([P, C * GB, N]),
                                            ALU.mult).then_inc(m2_done, 1)
                    dve.wait_ge(hi2_done, uno(u) + 1)
                    nc.vector.tensor_tensor(h2_lo[p][:, :, :], h2w[:, :, :], h2_hi[p][:, :, :].bitcast(F32),
                                            ALU.subtract).then_inc(lo2_done, 1)

                def out_add(t):
                    dve.wait_ge(yT_ready, t + 1)
                    dve.wait_ge(resb_done, t + 1)
                    wait(dve, out_stored, 16 * t)
                    nc.vector.tensor_tensor(out_sb[:, :, :], ps_t_y, resb[:, :, :], ALU.add).then_inc(out_done, 1)

                def first():
                    norm(0)
                    dve.wait_ge(bnst, 1)
                    aggregate(0)
                    nc.vector.tensor_reduce(feat[:, :], acc[:, :, :].rearrange("p b d -> p d b"), AX_X,
                                            ALU.add).then_inc(router, 1)
                    normalise(0)
                    dve.wait_ge(router_pe, 2)
                    nc.vector.tensor_tensor(logits[:, :], ps_l1[:, 1, 0:E], br_sb[:, :], ALU.add).then_inc(router, 1)
                    dve.wait_ge(router, 2)
                    nc.vector.tensor_reduce(neg_max[:, :], logits[:, :], AX_X, ALU.max, negate=True).then_inc(router, 2)
                    dve.wait_ge(router_act, 2)
                    nc.vector.reduce_sum(e_sum[:, :], e_w[:, :], AX_X).then_inc(router, 1)
                    dve.wait_ge(router, 5)
                    nc.vector.reciprocal(e_rinv[:, :], e_sum[:, :]).then_inc(router, 1)
                    dve.wait_ge(router, 6)
                    nc.vector.tensor_scalar(w_node[:, :], e_w[:, :], e_rinv[:, :], None, ALU.mult).then_inc(router, 1)
                    dve.wait_ge(router_act, 4)
                    x_low(0)
                    layer_1((0, 0))
                    layer_1((0, 1))
                    layer_2((0, 0))
                    layer_1((0, 2))
                    layer_2((0, 1))

                def body(t, last):
                    for u1, u2, u3, s in steps(t, last):
                        if s == 2 and not last:
                            norm(t + 1)
                            dve.wait_ge(bnst, t + 2)
                        if s == 3 and not last:
                            normalise(t + 1)
                        if u1:
                            layer_1(u1)
                        if s == E - 3 and not last:
                            x_low(t + 1)
                        if s == 2 and not last:
                            aggregate(t + 1)
                        if u2:
                            layer_2(u2)
                    out_add(t)

                over_tiles(dve, first, body)

            @block.tensor
            def _(pe):
                def product(acc_ps, i, src_hi, src_lo, m, start, stop):
                    cols = slice(m * P, (m + 1) * P)
                    terms = [(w, s, c) for c in range(C) for w, s in ((w_hi, src_hi), (w_hi, src_lo), (w_lo, src_hi))]
                    for n, (w, s, c) in enumerate(terms):
                        mm = nc.tensor.matmul(acc_ps, w[:, i, c, cols], s[:, c, :], start=start and n == 0,
                                              stop=stop and n == len(terms) - 1)
                    return mm

                def layer_1(u):
                    t, e = u
                    if e == 0:
                        pe.wait_ge(xlo_done, t + 1)
                    wait(pe, r1_done, uno(u))
                    for m in range(C):
                        product(ps_l1[:, m, :], e, xT_hi, xT_lo, m, True, True).then_inc(l1_done, 1)

                def layer_2(u):
                    e = u[1]
                    pe.wait_ge(lo1_done, uno(u) + 1)
                    wait(pe, r2_done, uno(u))
                    for m in range(C):
                        product(ps_l2[:, m, :], E + e, h1_hi[e % 2], h1_lo[e % 2], m, True, True).then_inc(l2_done, 1)

                def layer_3(u):
                    t, e = u
                    pe.wait_ge(lo2_done, uno(u) + 1)
                    if e == 0:
                        wait(pe, y_copied, t)
                    for m in range(C):
                        mm = product(ps_y[:, m, :], 2 * E + e, h2_hi[e % 2], h2_lo[e % 2], m, e == 0, e == E - 1)
                    mm.then_inc(l3_done, 1)

                def x_transpose(t):
                    pe.wait_ge(xnb_done, t + 1)
                    wait(pe, out_done, t - 1)
                    for c in range(C):
                        for b4 in range(GB):
                            last = nc.tensor.transpose(ps_t_x[:, c, b4 * N:(b4 + 1) * N],
                                                       xnb[:, b4, c * P:(c + 1) * P], ident[:, :])
                    last.then_inc(xT_ready, 1)

                def y_transpose(t):
                    pe.wait_ge(y_copied, t + 1)
                    pe.wait_ge(xlo_done, t + 2 if not (isinstance(t, int) and t == G - 1) else G)
                    for b4 in range(GB):
                        for m in range(C):
                            last = nc.tensor.transpose(ps_t_y[:, b4, m * P:(m + 1) * P],
                                                       yT[:, m, b4 * N:(b4 + 1) * N], ident[:, :])
                    last.then_inc(yT_ready, 1)

                def first():
                    pe.wait_ge(router, 1)
                    for c in range(C):
                        last = nc.tensor.transpose(ps_l1[:, 0, c * P:(c + 1) * P], feat[:, c * P:(c + 1) * P],
                                                   ident[:, :])
                    last.then_inc(router_pe, 1)
                    x_transpose(0)
                    pe.wait_ge(router_act, 1)
                    for c in range(C):
                        last = nc.tensor.matmul(ps_l1[:, 1, 0:E], featT[:, c, :], wr_sb[:, c, :],
                                                start=(c == 0), stop=(c == C - 1))
                    last.then_inc(router_pe, 1)
                    pe.wait_ge(router, 7)
                    w_out = ps_l2[:, :, :].rearrange("p c (e n) -> p (c e) n", n=P)
                    for e in range(E):
                        nc.tensor.matmul(w_out[:, e, :], w_node[:, e:e + 1].to_broadcast([P, P]), ident[:, :],
                                         start=True, stop=True)
                    nc.tensor.transpose(ps_y[0:E, 0, 0:P], w_node[:, :], ident[:, :]).then_inc(router_pe, 1)
                    pe.wait_ge(router_act, 4)
                    nc.tensor.matmul(ps_y[:, 1, 0:D], w_nodeT[:, :], bo_sb[:, :], start=True,
                                     stop=True).then_inc(router_pe, 1)
                    pe.wait_ge(router_act, 6)
                    layer_1((0, 0))
                    layer_1((0, 1))
                    layer_2((0, 0))
                    layer_1((0, 2))
                    layer_2((0, 1))
                    layer_3((0, 0))

                def body(t, last):
                    for u1, u2, u3, s in steps(t, last):
                        if u1:
                            layer_1(u1)
                        if s == 4 and not last:
                            x_transpose(t + 1)
                        if u2:
                            layer_2(u2)
                        if u3:
                            layer_3(u3)
                    y_transpose(t)

                over_tiles(pe, first, body)


_INS = ["x", "adj", "L0_gnn_W", "L0_gnn_a", "L0_ffn_Wr", "L0_ffn_br", "L0_ffn_W1", "L0_ffn_b1", "L0_ffn_g1",
        "L0_ffn_be1", "L0_ffn_m1", "L0_ffn_v1", "L0_ffn_W2", "L0_ffn_b2", "L0_ffn_g2", "L0_ffn_be2", "L0_ffn_m2",
        "L0_ffn_v2", "L0_ffn_Wo", "L0_ffn_bo"]


def kernel(**inputs):
    import numpy as _np
    import concourse.bacc as _bacc
    from concourse.bass_utils import run_bass_kernel_spmd as _run

    nc = _bacc.Bacc("TRN2", target_bir_lowering=False, num_devices=1)
    arrays, args = {}, []
    for name in _INS:
        a = _np.ascontiguousarray(inputs[name])
        arrays[f"in_{name}"] = a
        args.append(nc.dram_tensor(f"in_{name}", a.shape, mybir.dt.from_np(a.dtype), kind="ExternalInput").ap())
    out = nc.dram_tensor("out_0", inputs["x"].shape, F32, kind="ExternalOutput").ap()
    adj_ffn(nc, *args, out)
    r = _run(nc, [arrays], core_ids=[0])
    return r.results[0]["out_0"]
```

```python
from contextlib import ExitStack

import concourse.bass as bass
from concourse import mybir

F32 = mybir.dt.float32
F32R = mybir.dt.float32r
ALU = mybir.AluOpType
ACT = mybir.ActivationFunctionType
AX_X = mybir.AxisListType.X

P = 128
LN_EPS = 1e-5
ADJ_EPS = 1e-6
BN_EPS = 1e-3
SLOPE = 0.2


def wait(eng, sem, value):
    if isinstance(value, int) and value <= 0:
        return
    eng.wait_ge(sem, value)


def adj_ffn(nc, x, adj, gnn_w, gnn_a, wr, br, w1, b1, g1, be1, m1, v1, w2, b2, g2, be2, m2, v2, wo, bo, out):
    B, N, D = x.shape
    E = wr.shape[1]
    C = D // P
    GB = 4
    T = GB * N
    G = B // GB
    HB = GB // 2
    EC = E * C
    NW = 3 * E
    assert N == P and T == 512 and G % 2 == 0

    x_g = x.rearrange("(g b) n d -> g n b d", b=GB)
    adj_g = adj.rearrange("(g b) i j -> g i b j", b=GB)
    out_g = out.rearrange("(g b) n d -> g n b d", b=GB)
    x1_dram = nc.dram_tensor("x1_scratch", (G, P, GB * D), F32, kind="Internal").ap()

    with ExitStack() as ctx:
        def sb(name, shape, dt=F32, stack=ctx):
            return stack.enter_context(nc.sbuf_tensor(name, shape, dt))

        def sem(name, stack=ctx):
            return stack.enter_context(nc.semaphore(name))

        ident = sb("ident", [P, P])
        minus_half = sb("minus_half", [P, 2 * EC])
        eps_cols = sb("eps_cols", [P, GB])
        minus_one = sb("minus_one", [P, GB])
        w_hi = sb("w_hi", [P, NW, C, D], F32R)
        w_lo = sb("w_lo", [P, NW, C, D], F32R)
        bn_cols = sb("bn_cols", [P, 4, EC])
        acc = sb("acc", [P, GB, D])
        last_st = sb("last_st", [P, GB, 6])
        last_mv = sb("last_mv", [P, GB, 2])
        mean_rstd = sb("mean_rstd", [P, G, GB])
        wr_sb = sb("wr_sb", [P, C, E])
        br_sb = sb("br_sb", [P, E])
        bo_sb = sb("bo_sb", [E, D])

        x1 = [sb(f"x1_{i}", [P, GB, D]) for i in range(2)]
        rstd2 = [sb(f"rstd2_{i}", [P, GB]) for i in range(2)]
        x1t = sb("x1t", [P, GB, D])
        st = sb("st", [P, GB, 6])
        mv = sb("mv", [P, GB, 2])
        ve = sb("ve", [P, GB])
        rstd = sb("rstd", [P, GB])
        xnb = sb("xnb", [P, GB, D])
        xT_hi = sb("xT_hi", [P, C, T], F32R)
        xT_lo = sb("xT_lo", [P, C, T], F32R)

        ps_wide = ctx.enter_context(nc.psum_tensor("ps_wide", [P, 2 * C, T], F32))
        ps_l1 = ps_wide[:, 0:C, :]
        ps_l2 = ps_wide[:, C:2 * C, :]

        setup_done = sem("setup_done")
        l1_done = sem("l1_done")
        x1_stored = [sem(f"x1_stored{i}") for i in range(2)]
        last_bnst = sem("last_bnst")
        last_stats_done = sem("last_stats_done")
        acc_done = sem("acc_done")
        x1_loaded = sem("x1_loaded")
        bnst = sem("bnst")
        stats_done = sem("stats_done")
        ve_done = sem("ve_done")
        rstd_done = sem("rstd_done")
        xnb_done = sem("xnb_done")
        xT_ready = sem("xT_ready")
        xhi_done = sem("xhi_done")
        xlo_done = sem("xlo_done")

        def load_x1(sp, t):
            wait(sp, xnb_done, t)
            sp.dma_start(x1t[:, :, :].rearrange("p b d -> p (b d)"), x1_dram[t]).then_inc(x1_loaded, 16)

        def tile_stats(dve, t):
            dve.wait_ge(x1_loaded, 16 * (t + 1))
            for b4 in range(GB):
                last = nc.vector.bn_stats(st[:, b4, :], x1t[:, b4, :])
            last.then_inc(bnst, 1)

        def tile_aggregate(t):
            for b4 in range(GB):
                last = nc.vector.bn_aggr(mv[:, b4, :], st[:, b4, :])
            last.then_inc(stats_done, 1)

        def tile_rstd(pool, t):
            pool.wait_ge(stats_done, t + 1)
            nc.gpsimd.tensor_tensor(ve[:, :], mv[:, :, 1], eps_cols[:, :], ALU.add).then_inc(ve_done, 1)
            pool.wait_ge(ve_done, t + 1)
            nc.gpsimd.tensor_tensor(rstd[:, :], ve[:, :], minus_half[:, 0:GB], ALU.pow).then_inc(rstd_done, 1)

        def tile_normalise(dve, t):
            dve.wait_ge(rstd_done, t + 1)
            dve.wait_ge(stats_done, t + 1)
            for b4 in range(GB):
                last = nc.vector.tensor_scalar(xnb[:, b4, :], x1t[:, b4, :], mv[:, b4, 0:1],
                                               rstd[:, b4:b4 + 1], ALU.subtract, ALU.mult)
            last.then_inc(xnb_done, 1)

        def tile_transpose(pe, t, ps_x):
            pe.wait_ge(xnb_done, t + 1)
            for c in range(C):
                for b4 in range(GB):
                    last = nc.tensor.transpose(ps_x[:, c, b4 * N:(b4 + 1) * N], xnb[:, b4, c * P:(c + 1) * P],
                                               ident[:, :])
            last.then_inc(xT_ready, 1)

        def tile_high(act, t, ps_x):
            act.wait_ge(xT_ready, t + 1)
            nc.scalar.activation(xT_hi[:, :, :], ps_x, ACT.Copy).then_inc(xhi_done, 1)

        def product(acc_ps, i, src_hi, src_lo, m, start, stop):
            cols = slice(m * P, (m + 1) * P)
            terms = [(w, s, c) for c in range(C) for w, s in ((w_hi, src_hi), (w_hi, src_lo), (w_lo, src_hi))]
            for n, (w, s, c) in enumerate(terms):
                mm = nc.tensor.matmul(acc_ps, w[:, i, c, cols], s[:, c, :], start=start and n == 0,
                                      stop=stop and n == len(terms) - 1)
            return mm

        def add_group(p):
            for b4 in range(GB):
                last = nc.vector.scalar_tensor_tensor(out=acc[:, b4, :], in0=x1[p][:, b4, :],
                                                      scalar=rstd2[p][:, b4:b4 + 1], in1=acc[:, b4, :],
                                                      op0=ALU.mult, op1=ALU.add)
            last.then_inc(acc_done, 1)

        def tile_low(dve, t, ps_x):
            dve.wait_ge(xhi_done, t + 1)
            nc.vector.tensor_tensor(xT_lo[:, :, :], ps_x, xT_hi[:, :, :].bitcast(F32),
                                    ALU.subtract).then_inc(xlo_done, 1)

        with ExitStack() as sa:
            def sba(name, shape, dt=F32):
                return sb(name, shape, dt, sa)

            def ps(name, shape):
                return sa.enter_context(nc.psum_tensor(name, shape, F32))

            w_stage = [sba(f"w_stage{i}", [P, C, D]) for i in range(2)]
            bn_rows = sba("bn_rows", [EC, 2, 5, P])
            bn_in = sba("bn_in", [P, 2, 5, EC])
            bn_tmp = sba("bn_tmp", [P, 4, 2, EC])
            a_rows = sba("a_rows", [2 * C, P])
            a_cols = sba("a_cols", [P, 2 * C])
            gw = sba("gw", [P, C, D + 2])
            gwT = sba("gwT", [P, C, D])
            x_sb = [sba(f"x_sb{i}", [P, GB, D]) for i in range(2)]
            res = [sba(f"res{i}", [P, GB, D]) for i in range(2)]
            adj_sb = [sba(f"adj_sb{i}", [P, GB, N]) for i in range(2)]
            st1 = sba("st1", [P, GB, 6])
            mv1 = [sba(f"mv1_{i}", [P, GB, 2]) for i in range(2)]
            ve1 = sba("ve1", [P, GB])
            neg_mean1 = sba("neg_mean1", [P, GB])
            nb1 = [sba(f"nb1_{i}", [P, GB]) for i in range(2)]
            rstd1 = [sba(f"rstd1_{i}", [P, GB]) for i in range(2)]
            xn = sba("xn", [P, GB, D])
            xnT = sba("xnT", [P, C, T])
            wh = [sba(f"wh{i}", [P, GB, D + 2]) for i in range(2)]
            s2max = sba("s2max", [P, GB])
            neg_u = sba("neg_u", [P, GB])
            neg_m = sba("neg_m", [P, GB])
            exp_bias = [sba(f"exp_bias{i}", [P, 2, GB]) for i in range(2)]
            e_sb = sba("e_sb", [P, 2, GB, N])
            e_max = sba("e_max", [P, GB, N])
            p_sb = sba("p_sb", [P, GB, N])
            pT = sba("pT", [P, GB, N])
            rowsum = sba("rowsum", [P, GB])
            rinv = sba("rinv", [P, GB])
            st2 = sba("st2", [P, GB, 6])
            mv2 = [sba(f"mv2_{i}", [P, GB, 2]) for i in range(2)]
            ve2 = sba("ve2", [P, GB])
            x1s_low = sba("x1s_low", [P, HB, D])
            x1s_high = sba("x1s_high", [P, HB, D])

            ps_th = ps("ps_th", [P, GB * D])
            ps_xT = ps_th[:, :].rearrange("p (c t) -> p c t", c=C)
            ps_h = ps_th[:, :].rearrange("p (b d) -> p b d", b=GB)
            ps_pT = ps("ps_pT", [P, GB, N])
            ps_s = ps("ps_s", [P, GB, N])
            ps_bn = ps_pT[:, :, :].rearrange("p b n -> p (b n)")[:, 0:10 * EC].rearrange("p (r k) -> p r k", k=EC)

            w_loaded = [sem(f"w_loaded{i}", sa) for i in range(2)]
            w_hi_done = sem("w_hi_done", sa)
            w_slots_free = sem("w_slots_free", sa)
            proj_loaded = sem("proj_loaded", sa)
            small_loaded = sem("small_loaded", sa)
            bn_step = sem("bn_step", sa)
            proj_T = sem("proj_T", sa)
            proj_T_copied = sem("proj_T_copied", sa)
            va_ready = sem("va_ready", sa)
            va_copied = sem("va_copied", sa)
            bn_T = sem("bn_T", sa)
            bn_copied = sem("bn_copied", sa)
            x_loaded = [sem(f"x_loaded{i}", sa) for i in range(2)]
            res_loaded = [sem(f"res_loaded{i}", sa) for i in range(2)]
            adj_loaded = [sem(f"adj_loaded{i}", sa) for i in range(2)]
            bnst1 = sem("bnst1", sa)
            stats1_done = sem("stats1_done", sa)
            ve1_done = sem("ve1_done", sa)
            rstd1_done = sem("rstd1_done", sa)
            nb1_done = sem("nb1_done", sa)
            xn_done = sem("xn_done", sa)
            xnT_ready = sem("xnT_ready", sa)
            xnT_copied = sem("xnT_copied", sa)
            wh_ready = sem("wh_ready", sa)
            wh_copied = sem("wh_copied", sa)
            s2b_ready = sem("s2b_ready", sa)
            s2max_done = sem("s2max_done", sa)
            neg_u_done = sem("neg_u_done", sa)
            neg_m_done = sem("neg_m_done", sa)
            bias_done = sem("bias_done", sa)
            e_max_done = sem("e_max_done", sa)
            e_done = sem("e_done", sa)
            p_done = sem("p_done", sa)
            pT_ready = sem("pT_ready", sa)
            pT_copied = sem("pT_copied", sa)
            h_low_ready = sem("h_low_ready", sa)
            h_ready = sem("h_ready", sa)
            rowsum_done = sem("rowsum_done", sa)
            rinv_done = sem("rinv_done", sa)
            x1_low_done = sem("x1_low_done", sa)
            x1_done = sem("x1_done", sa)
            bnst2 = sem("bnst2", sa)
            stats2_done = sem("stats2_done", sa)
            ve2_done = sem("ve2_done", sa)
            rstd2_done = sem("rstd2_done", sa)
            x1s_low_done = sem("x1s_low_done", sa)
            x1s_high_done = sem("x1s_high_done", sa)
            acc_low_done = sem("acc_low_done", sa)
            acc_high_done = sem("acc_high_done", sa)
            N_SMALL = 2 * 5 + 3

            K0, K1 = 3, G // 2 - 1
            assert 2 * (K1 - K0) == NW and E % 2 == 0

            w_dram = [w.rearrange("e (c p) n -> e p c n", p=P) for w in (w1, w2, wo)]

            def num(g):
                return 2 * g[0] + g[1]

            def ago(g, n):
                q = g[1] - n
                return (g[0] + q // 2, q % 2)

            def exists(g):
                return not isinstance(g[0], int) or 0 <= num(g) < G

            def over_groups(eng, step):
                for i in range(-2, 2 * K0):
                    step((i // 2, i % 2))
                with eng.Fori(K0, K1) as k:
                    step((k, 0))
                    step((k, 1))
                for i in range(2 * K1, G + 2):
                    step((i // 2, i % 2))

            def is_step(g, n):
                return isinstance(g[0], int) and num(g) == n

            BN_STEP = 0
            ps_x0 = ps_l2

            def matrix(g):
                i = num(g) - 2 * K0
                return i if not isinstance(i, int) or 0 <= i < NW else None

            block = sa.enter_context(nc.Block())

            @block.sync
            def _(sp):
                def load_x(g):
                    p = g[1]
                    wait(sp, xn_done, num(g) - 1)
                    sp.dma_start(x_sb[p][:, :, :], x_g[num(g)]).then_inc(x_loaded[p], 16)

                load_x((0, 0))
                sp.dma_start(gw[:, :, 0:D], gnn_w.rearrange("(c p) n -> p c n", p=P)).then_inc(proj_loaded, 16)
                sp.dma_start(a_rows[:, :], gnn_a.rearrange("(r p) o -> r (p o)", p=P)).then_inc(proj_loaded, 16)
                load_x((0, 1))
                for layer, rows in enumerate(((g1, b1, be1, m1, v1), (g2, b2, be2, m2, v2))):
                    for i, r in enumerate(rows):
                        sp.dma_start(bn_rows[:, layer, i, :],
                                     r.rearrange("e (c p) -> (e c) p", p=P)).then_inc(small_loaded, 16)
                sp.dma_start(wr_sb[:, :, :], wr.rearrange("(c p) e -> p c e", p=P)).then_inc(small_loaded, 16)
                sp.dma_start(br_sb[:, :], br.partition_broadcast(P)).then_inc(small_loaded, 16)
                sp.dma_start(bo_sb[:, :], bo).then_inc(small_loaded, 16)

                def step(g, layer=None):
                    p = g[1]
                    if exists(ago(g, -2)):
                        load_x(ago(g, -2))
                    b = ago(g, 3)
                    if exists(b):
                        wait(sp, x1_done, num(b) + 1)
                        sp.dma_start(x1_dram[num(b)], x1[b[1]][:, :, :].rearrange("p b d -> p (b d)")
                                     ).then_inc(x1_stored[b[1]], 16)
                    r = ago(g, 1)
                    if exists(r):
                        wait(sp, x1_done, num(r) - 1)
                        sp.dma_start(res[r[1]][:, :, :], x_g[num(r)]).then_inc(res_loaded[r[1]], 16)
                    if exists(g):
                        wait(sp, p_done, num(g) - 1)
                        sp.dma_start(adj_sb[p][:, :, :], adj_g[num(g)]).then_inc(adj_loaded[p], 16)
                    if layer is not None:
                        i = matrix(g)
                        sp.wait_ge(w_slots_free, i + 1)
                        sp.dma_start(w_stage[p][:, :, :], w_dram[layer][i - layer * E]).then_inc(w_loaded[p], 16)
                    if is_step(g, 2 * K0 - 1):
                        sp.wait_ge(x1_stored[0], 16)
                        load_x1(sp, 0)

                for i in range(2 * K0):
                    step((i // 2, i % 2))
                for layer in range(3):
                    with sp.Fori(K0 + layer * E // 2, K0 + (layer + 1) * E // 2) as k:
                        step((k, 0), layer)
                        step((k, 1), layer)
                for i in range(2 * K1, G + 3):
                    step((i // 2, i % 2))

            @block.gpsimd
            def _(pool):
                nc.gpsimd.memset(ident[:, :], 0.0).then_inc(bn_step, 1)
                nc.gpsimd.memset(minus_half[:, :], -0.5).then_inc(w_slots_free, 2)
                nc.gpsimd.memset(eps_cols[:, :], LN_EPS)
                nc.gpsimd.memset(minus_one[:, :], -1.0)
                nc.gpsimd.memset(acc[:, :, :], 0.0)
                pool.wait_ge(bn_step, 1)
                nc.gpsimd.affine_select(out=ident[:, :], in_=ident[:, :], compare_op=ALU.not_equal, fill=1.0,
                                        base=0, pattern=[[-1, P]], channel_multiplier=1).then_inc(setup_done, 1)
                pool.wait_ge(setup_done, 1)

                def rstd_1(g):
                    p = g[1]
                    pool.wait_ge(stats1_done, num(g) + 1)
                    wait(pool, nb1_done, num(g))
                    nc.gpsimd.tensor_tensor(ve1[:, :], mv1[p][:, :, 1], eps_cols[:, :], ALU.add)
                    nc.gpsimd.tensor_tensor(neg_mean1[:, :], mv1[p][:, :, 0], minus_one[:, :],
                                            ALU.mult).then_inc(ve1_done, 1)
                    pool.wait_ge(ve1_done, num(g) + 1)
                    nc.gpsimd.tensor_tensor(rstd1[p][:, :], ve1[:, :], minus_half[:, 0:GB],
                                            ALU.pow).then_inc(rstd1_done, 1)
                    pool.wait_ge(rstd1_done, num(g) + 1)
                    nc.gpsimd.tensor_tensor(nb1[p][:, :], neg_mean1[:, :], rstd1[p][:, :],
                                            ALU.mult).then_inc(nb1_done, 1)

                def batch_norm_constants():
                    pool.wait_ge(bn_copied, 1)
                    exps = minus_half[:, :].rearrange("p (l n) -> p l n", l=2)
                    scale = bn_cols[:, 0:4:2, :]
                    shift = bn_cols[:, 1:4:2, :]
                    nc.gpsimd.tensor_scalar(bn_tmp[:, 0], bn_in[:, :, 4, :], BN_EPS, None, ALU.add).then_inc(bn_step, 1)
                    nc.gpsimd.tensor_tensor(bn_tmp[:, 2], bn_in[:, :, 1, :], bn_in[:, :, 3, :],
                                            ALU.subtract).then_inc(bn_step, 1)
                    pool.wait_ge(bn_step, 3)
                    nc.gpsimd.tensor_tensor(bn_tmp[:, 1], bn_tmp[:, 0], exps, ALU.pow).then_inc(bn_step, 1)
                    pool.wait_ge(bn_step, 4)
                    nc.gpsimd.tensor_tensor(scale, bn_in[:, :, 0, :], bn_tmp[:, 1], ALU.mult).then_inc(bn_step, 1)
                    pool.wait_ge(bn_step, 5)
                    nc.gpsimd.tensor_tensor(bn_tmp[:, 3], bn_tmp[:, 2], scale, ALU.mult).then_inc(bn_step, 1)
                    pool.wait_ge(bn_step, 6)
                    nc.gpsimd.tensor_tensor(shift, bn_tmp[:, 3], bn_in[:, :, 2, :], ALU.add)

                def step(g):
                    nxt = ago(g, -2)
                    if exists(nxt):
                        rstd_1(nxt)
                    if is_step(g, BN_STEP):
                        batch_norm_constants()
                    if is_step(g, G - 2):
                        tile_rstd(pool, 0)
                    h = ago(g, 4)
                    if exists(h):
                        pool.wait_ge(x1s_low_done, num(h) + 1)
                        wait(pool, acc_low_done, num(h))
                        nc.gpsimd.tensor_tensor(acc[:, :HB, :], acc[:, :HB, :], x1s_low[:, :, :],
                                                ALU.add).then_inc(acc_low_done, 1)
                    t = ago(g, 3)
                    if exists(t):
                        p = t[1]
                        pool.wait_ge(stats2_done, num(t) + 1)
                        wait(pool, acc_high_done, num(t))
                        nc.gpsimd.tensor_tensor(ve2[:, :], mv2[p][:, :, 1], eps_cols[:, :],
                                                ALU.add).then_inc(ve2_done, 1)
                        pool.wait_ge(ve2_done, num(t) + 1)
                        nc.gpsimd.tensor_tensor(rstd2[p][:, :], ve2[:, :], minus_half[:, 0:GB],
                                                ALU.pow).then_inc(rstd2_done, 1)
                        pool.wait_ge(rstd2_done, num(t) + 1)
                        nc.gpsimd.tensor_tensor(mean_rstd[:, num(t), :], mv2[p][:, :, 0], rstd2[p][:, :],
                                                ALU.mult)
                    if exists(t) and not is_step(t, G - 2):
                        wait(pool, acc_high_done, num(t))
                        nc.gpsimd.tensor_tensor(x1s_high[:, :, :], x1[p][:, HB:, :],
                                                rstd2[p][:, HB:, None].to_broadcast([P, HB, D]),
                                                ALU.mult).then_inc(x1s_high_done, 1)
                        pool.wait_ge(x1s_high_done, num(t) + 1)
                        nc.gpsimd.tensor_tensor(acc[:, HB:, :], acc[:, HB:, :], x1s_high[:, :, :],
                                                ALU.add).then_inc(acc_high_done, 1)
                    i = matrix(g)
                    if i is not None:
                        pool.wait_ge(w_hi_done, i + 1)
                        nc.gpsimd.tensor_tensor(w_lo[:, i, :, :], w_stage[g[1]][:, :, :],
                                                w_hi[:, i, :, :].bitcast(F32), ALU.subtract).then_inc(w_slots_free, 1)

                over_groups(pool, step)

            @block.scalar
            def _(act):
                act.wait_ge(proj_T, 1)
                nc.scalar.activation(gwT[:, :, :], ps_h[:, 0:C, :], ACT.Copy)
                nc.scalar.activation(a_cols[:, :], ps_s[:, 0, 0:2 * C], ACT.Copy).then_inc(proj_T_copied, 1)
                act.wait_ge(va_ready, 1)
                nc.scalar.activation(gw[:, :, D:D + 2], ps_s[:, 1, 0:2 * C].rearrange("p (c k) -> p c k", k=2),
                                     ACT.Copy).then_inc(va_copied, 1)

                def normalise(g):
                    p = g[1]
                    act.wait_ge(nb1_done, num(g) + 1)
                    wait(act, xnT_ready, num(g))
                    for b4 in range(GB):
                        last = nc.scalar.activation(xn[:, b4, :], x_sb[p][:, b4, :], ACT.Identity,
                                                    bias=nb1[p][:, b4:b4 + 1], scale=rstd1[p][:, b4:b4 + 1])
                    last.then_inc(xn_done, 1)

                def step(g):
                    p = g[1]
                    b = ago(g, 2)
                    if exists(b):
                        act.wait_ge(pT_ready, num(b) + 1)
                        wait(act, h_ready, num(b))
                        nc.scalar.activation(pT[:, :, :], ps_pT[:, :, :], ACT.Copy).then_inc(pT_copied, 1)
                    t = ago(g, 4)
                    if exists(t):
                        act.wait_ge(rstd2_done, num(t) + 1)
                        wait(act, acc_low_done, num(t))
                        for b4 in range(HB):
                            last = nc.scalar.activation(x1s_low[:, b4, :], x1[t[1]][:, b4, :], ACT.Copy,
                                                        scale=rstd2[t[1]][:, b4:b4 + 1])
                        last.then_inc(x1s_low_done, 1)
                    nxt = ago(g, -1)
                    if exists(nxt):
                        normalise(nxt)
                    a = ago(g, 1)
                    if exists(a):
                        r = a[1]
                        act.wait_ge(bias_done, num(a) + 1)
                        wait(act, e_max_done, num(a))
                        for b4 in range(GB):
                            nc.scalar.activation(e_sb[:, 0, b4, :], ps_s[:, b4, :], ACT.Exp,
                                                 bias=exp_bias[r][:, 0, b4:b4 + 1])
                            last = nc.scalar.activation(e_sb[:, 1, b4, :], ps_s[:, b4, :], ACT.Exp,
                                                        bias=exp_bias[r][:, 1, b4:b4 + 1], scale=SLOPE)
                        last.then_inc(e_done, 1)
                    if is_step(g, BN_STEP - 1):
                        act.wait_ge(bn_T, 1)
                        nc.scalar.activation(bn_in[:, :, :, :].rearrange("p l i k -> p (l i) k"), ps_bn,
                                             ACT.Copy).then_inc(bn_copied, 1)
                    if is_step(g, G):
                        tile_high(act, 0, ps_x0)
                    i = matrix(g)
                    if i is not None:
                        act.wait_ge(w_loaded[p], 16 * (g[0] - K0 + 1))
                        nc.scalar.activation(w_hi[:, i, :, :], w_stage[p][:, :, :], ACT.Copy).then_inc(w_hi_done, 1)
                    if exists(g):
                        act.wait_ge(wh_ready, num(g) + 1)
                        wait(act, h_ready, num(g) - 1)
                        nc.scalar.activation(wh[p][:, :, :], ps_wide[:, :, 0:D + 2], ACT.Copy).then_inc(wh_copied, 1)
                    if exists(nxt):
                        act.wait_ge(xnT_ready, num(nxt) + 1)
                        wait(act, wh_ready, num(nxt))
                        nc.scalar.activation(xnT[:, :, :], ps_xT, ACT.Copy).then_inc(xnT_copied, 1)

                over_groups(act, step)

            @block.vector
            def _(dve):
                def stats_1(g, b4):
                    if b4 == 0:
                        wait(dve, stats1_done, num(g))
                        dve.wait_ge(x_loaded[g[1]], 16 * (g[0] + 1))
                    part = nc.vector.bn_stats(st1[:, b4, :], x_sb[g[1]][:, b4, :])
                    if b4 == GB - 1:
                        part.then_inc(bnst1, 1)

                def stats_2(g, b4):
                    if b4 == 0:
                        wait(dve, stats2_done, num(g))
                        dve.wait_ge(x1_done, num(g) + 1)
                    part = nc.vector.bn_stats(st2[:, b4, :], x1[g[1]][:, b4, :])
                    if b4 == GB - 1:
                        part.then_inc(bnst2, 1)

                def aggregate_1(g):
                    for b4 in range(GB):
                        last = nc.vector.bn_aggr(mv1[g[1]][:, b4, :], st1[:, b4, :])
                    last.then_inc(stats1_done, 1)

                def aggregate_2(g):
                    for b4 in range(GB):
                        last = nc.vector.bn_aggr(mv2[g[1]][:, b4, :], st2[:, b4, :])
                    last.then_inc(stats2_done, 1)

                def step(g):
                    p = g[1]
                    a = ago(g, 1)
                    r = a[1]
                    nxt = ago(g, -2)

                    def stats_part(b4):
                        if exists(nxt):
                            stats_1(nxt, b4)

                    if exists(a):
                        dve.wait_ge(s2b_ready, num(a) + 1)
                        nc.vector.tensor_reduce(s2max[:, :], ps_s[:, :, :], AX_X, ALU.max).then_inc(s2max_done, 1)
                        stats_part(0)
                        dve.wait_ge(s2max_done, num(a) + 1)
                        nc.vector.scalar_tensor_tensor(out=neg_u[:, :], in0=s2max[:, :], scalar=-1.0,
                                                       in1=wh[r][:, :, D], op0=ALU.mult,
                                                       op1=ALU.subtract).then_inc(neg_u_done, 1)
                        stats_part(1)
                        dve.wait_ge(neg_u_done, num(a) + 1)
                        nc.vector.scalar_tensor_tensor(out=neg_m[:, :], in0=neg_u[:, :], scalar=SLOPE,
                                                       in1=neg_u[:, :], op0=ALU.mult,
                                                       op1=ALU.min).then_inc(neg_m_done, 1)
                        stats_part(2)
                        dve.wait_ge(neg_m_done, num(a) + 1)
                        wait(dve, e_done, num(a) - 1)
                        nc.vector.tensor_tensor(exp_bias[r][:, 0, :], wh[r][:, :, D], neg_m[:, :], ALU.add)
                        nc.vector.scalar_tensor_tensor(out=exp_bias[r][:, 1, :], in0=wh[r][:, :, D], scalar=SLOPE,
                                                       in1=neg_m[:, :], op0=ALU.mult,
                                                       op1=ALU.add).then_inc(bias_done, 1)
                        stats_part(3)
                    else:
                        for b4 in range(GB):
                            stats_part(b4)
                    if is_step(g, G - 2):
                        tile_stats(dve, 0)
                        dve.wait_ge(bnst, 1)
                        tile_aggregate(0)
                    if is_step(g, G - 1):
                        tile_normalise(dve, 0)
                    b = ago(g, 2)
                    q = b[1]
                    t = ago(g, 3)
                    if exists(nxt):
                        dve.wait_ge(bnst1, num(nxt) + 1)
                    elif exists(b):
                        dve.wait_ge(rowsum_done, num(b) + 1)
                        if exists(t):
                            dve.wait_ge(bnst2, num(t) + 1)
                    elif exists(t):
                        dve.wait_ge(bnst2, num(t) + 1)
                    if exists(b):
                        nc.vector.reciprocal(rinv[:, :], rowsum[:, :]).then_inc(rinv_done, 1)
                    if exists(nxt):
                        aggregate_1(nxt)
                    if exists(t):
                        aggregate_2(t)
                    if exists(b):
                        dve.wait_ge(h_low_ready, num(b) + 1)
                        dve.wait_ge(rinv_done, num(b) + 1)
                        dve.wait_ge(res_loaded[q], 16 * (b[0] + 1))
                        wait(dve, x1_stored[q], 16 * b[0])
                        wait(dve, x1s_low_done, num(b) - 1)
                        wait(dve, x1s_high_done, num(b) - 1)
                        for b4 in range(GB):
                            if b4 == HB:
                                dve.wait_ge(h_ready, num(b) + 1)
                            last = nc.vector.scalar_tensor_tensor(out=x1[q][:, b4, :], in0=ps_h[:, b4, :],
                                                                  scalar=rinv[:, b4:b4 + 1], in1=res[q][:, b4, :],
                                                                  op0=ALU.mult, op1=ALU.add)
                            if b4 == HB - 1:
                                last.then_inc(x1_low_done, 1)
                        last.then_inc(x1_done, 1)
                    with_stats = exists(b) and not is_step(b, G - 1)
                    if exists(a):
                        dve.wait_ge(e_done, num(a) + 1)
                        nc.vector.tensor_tensor(e_max[:, :, :], e_sb[:, 0, :, :], e_sb[:, 1, :, :],
                                                ALU.max).then_inc(e_max_done, 1)
                        if with_stats:
                            stats_2(b, 0)
                        dve.wait_ge(e_max_done, num(a) + 1)
                        dve.wait_ge(adj_loaded[r], 16 * (a[0] + 1))
                        wait(dve, pT_ready, num(a))
                        nc.vector.scalar_tensor_tensor(out=p_sb[:, :, :], in0=adj_sb[r][:, :, :], scalar=ADJ_EPS,
                                                       in1=e_max[:, :, :], op0=ALU.add,
                                                       op1=ALU.mult).then_inc(p_done, 1)
                        if with_stats:
                            stats_2(b, 1)
                        if is_step(g, G):
                            tile_low(dve, 0, ps_x0)
                        dve.wait_ge(p_done, num(a) + 1)
                        wait(dve, rinv_done, num(a))
                        nc.vector.tensor_reduce(rowsum[:, :], p_sb[:, :, :], AX_X, ALU.add).then_inc(rowsum_done, 1)
                    if with_stats:
                        for b4 in range(2 if exists(a) else 0, GB):
                            stats_2(b, b4)

                over_groups(dve, step)
                dve.wait_ge(x1_done, G)
                for b4 in range(GB):
                    last = nc.vector.bn_stats(last_st[:, b4, :], x1[(G - 1) % 2][:, b4, :])
                last.then_inc(last_bnst, 1)
                dve.wait_ge(last_bnst, 1)
                for b4 in range(GB):
                    last = nc.vector.bn_aggr(last_mv[:, b4, :], last_st[:, b4, :])
                last.then_inc(last_stats_done, 1)
                dve.wait_ge(acc_low_done, G - 2)
                dve.wait_ge(acc_high_done, G - 2)
                dve.wait_ge(rstd2_done, G - 1)
                add_group((G - 2) % 2)

            @block.tensor
            def _(pe):
                pe.wait_ge(setup_done, 1)
                pe.wait_ge(proj_loaded, 2 * 16)
                for m in range(C):
                    for c in range(C):
                        nc.tensor.transpose(ps_h[:, m, c * P:(c + 1) * P], gw[:, c, m * P:(m + 1) * P], ident[:, :])
                nc.tensor.transpose(ps_s[:, 0, 0:2 * C], a_rows[:, :], ident[0:2 * C, 0:2 * C]).then_inc(proj_T, 1)
                pe.wait_ge(proj_T_copied, 1)
                a_pair = a_cols[:, :].rearrange("p (k m) -> p m k", k=2)
                for c in range(C):
                    for m in range(C):
                        last = nc.tensor.matmul(ps_s[:, 1, 2 * c:2 * c + 2], gwT[:, m, c * P:(c + 1) * P],
                                                a_pair[:, m, :], start=(m == 0), stop=(m == C - 1))
                last.then_inc(va_ready, 1)

                def project(g, graphs):
                    for b4 in graphs:
                        for c in range(C):
                            mm = nc.tensor.matmul(ps_wide[:, b4, 0:D + 2], xnT[:, c, b4 * N:(b4 + 1) * N],
                                                  gw[:, c, :], start=(c == 0), stop=(c == C - 1))
                    return mm

                def step(g):
                    a = ago(g, 1)
                    b = ago(g, 2)
                    nxt = ago(g, -1)
                    if exists(b):
                        pe.wait_ge(p_done, num(b) + 1)
                        wait(pe, pT_copied, num(b))
                        for b4 in range(GB):
                            last = nc.tensor.transpose(ps_pT[:, b4, :], p_sb[:, b4, :], ident[:, :])
                        last.then_inc(pT_ready, 1)
                    if exists(a):
                        pe.wait_ge(wh_copied, num(a) + 1)
                        wait(pe, e_done, num(a))
                        wait(pe, s2max_done, num(a))
                        for b4 in range(GB):
                            last = nc.tensor.matmul(ps_s[:, b4, :], wh[a[1]][:, b4, D + 1:D + 2].to_broadcast([P, P]),
                                                    ident[:, :], start=True, stop=True)
                        last.then_inc(s2b_ready, 1)
                    if is_step(g, G):
                        pe.wait_ge(wh_copied, G)
                        tile_transpose(pe, 0, ps_x0)
                    if is_step(g, 0):
                        pe.wait_ge(va_copied, 1)
                    if exists(g):
                        pe.wait_ge(xnT_copied, num(g) + 1)
                        wait(pe, wh_copied, num(g))
                        project(g, range(GB // 2))
                    if exists(b):
                        pe.wait_ge(pT_copied, num(b) + 1)
                        pe.wait_ge(wh_copied, num(b) + 1)
                        wait(pe, x1_done, num(b))
                        pe.wait_ge(xnT_copied, min(num(g) + 1, G) if isinstance(g[0], int) else num(g) + 1)
                        for b4 in range(GB):
                            last = nc.tensor.matmul(ps_h[:, b4, :], pT[:, b4, :], wh[b[1]][:, b4, 0:D], start=True,
                                                    stop=True)
                            if b4 == HB - 1:
                                last.then_inc(h_low_ready, 1)
                        last.then_inc(h_ready, 1)
                    if exists(g):
                        project(g, range(GB // 2, GB)).then_inc(wh_ready, 1)
                    if exists(nxt):
                        pe.wait_ge(xn_done, num(nxt) + 1)
                        wait(pe, xnT_copied, num(nxt))
                        for c in range(C):
                            wait(pe, (x1_low_done, x1_done)[c], num(b) + 1)
                            for b4 in range(GB):
                                last = nc.tensor.transpose(ps_xT[:, c, b4 * N:(b4 + 1) * N],
                                                           xn[:, b4, c * P:(c + 1) * P], ident[:, :])
                        last.then_inc(xnT_ready, 1)
                    if is_step(g, BN_STEP - 1):
                        pe.wait_ge(small_loaded, 16 * N_SMALL)
                        for r in range(10):
                            last = nc.tensor.transpose(ps_bn[:, r, :], bn_rows[:, r // 5, r % 5, :],
                                                       ident[0:EC, 0:EC])
                        last.then_inc(bn_T, 1)

                over_groups(pe, step)
                pe.wait_ge(xlo_done, 1)
                for m in range(C):
                    product(ps_l1[:, m, :], 0, xT_hi, xT_lo, m, True, True).then_inc(l1_done, 1)

        with ExitStack() as sbk:
            def sbb(name, shape, dt=F32):
                return sb(name, shape, dt, sbk)

            def psb(name, shape):
                return sbk.enter_context(nc.psum_tensor(name, shape, F32))

            last_ve = sbb("last_ve", [P, GB])
            feat_sum = sbb("feat_sum", [P, D])
            mean_sum = sbb("mean_sum", [P, 1])
            feat = sbb("feat", [P, D])
            featT = sbb("featT", [P, C, P])
            logits = sbb("logits", [P, E])
            neg_max = sbb("neg_max", [P, 1])
            e_w = sbb("e_w", [P, E])
            e_sum = sbb("e_sum", [P, 1])
            e_rinv = sbb("e_rinv", [P, 1])
            w_node = sbb("w_node", [P, E])
            w_nodeT = sbb("w_nodeT", [E, P])
            w_bc = sbb("w_bc", [P, E, P])
            bias_out = sbb("bias_out", [P, D])
            h1 = sbb("h1", [P, C, T])
            h1_hi = [sbb(f"h1_hi{i}", [P, C, T], F32R) for i in range(2)]
            h1_lo = [sbb(f"h1_lo{i}", [P, C, T], F32R) for i in range(2)]
            h2 = sbb("h2", [P, C, T])
            h2w = sbb("h2w", [P, C, T])
            h2_hi = [sbb(f"h2_hi{i}", [P, C, T], F32R) for i in range(2)]
            h2_lo = [sbb(f"h2_lo{i}", [P, C, T], F32R) for i in range(2)]
            resb = sbb("resb", [P, GB, D])
            out_sb = sbb("out_sb", [P, GB, D])

            ps_y = psb("ps_y", [P, GB, D])
            ps_t = psb("ps_t", [P, C * T])
            ps_t_x = ps_t[:, :].rearrange("p (c n) -> p c n", c=C)

            def semb(name):
                return sem(name, sbk)

            last_ve_done = semb("last_ve_done")
            last_rstd_done = semb("last_rstd_done")
            mean_rstd_done = semb("mean_rstd_done")
            feat_sum_done = semb("feat_sum_done")
            feat_done = semb("feat_done")
            featT_ready = semb("featT_ready")
            featT_copied = semb("featT_copied")
            logits_ready = semb("logits_ready")
            logits_done = semb("logits_done")
            neg_max_done = semb("neg_max_done")
            e_w_done = semb("e_w_done")
            e_sum_done = semb("e_sum_done")
            e_rinv_done = semb("e_rinv_done")
            w_node_done = semb("w_node_done")
            w_rows_ready = semb("w_rows_ready")
            w_bc_done = semb("w_bc_done")
            w_nodeT_ready = semb("w_nodeT_ready")
            w_nodeT_copied = semb("w_nodeT_copied")
            bias_ready = semb("bias_ready")
            bias_out_done = semb("bias_out_done")
            r1_done = semb("r1_done")
            hi1_done = semb("hi1_done")
            lo1_done = semb("lo1_done")
            l2_done = semb("l2_done")
            r2_done = semb("r2_done")
            m2_done = semb("m2_done")
            hi2_done = semb("hi2_done")
            lo2_done = semb("lo2_done")
            l3_done = semb("l3_done")
            res_loaded_b = semb("res_loaded_b")
            resb_done = semb("resb_done")
            out_done = semb("out_done")
            out_stored = semb("out_stored")

            def unit(t, e):
                return (t + e // E, e % E)

            def uno(u):
                return E * u[0] + u[1]

            def over_tiles(eng, first, body):
                first()
                body(0, False)
                with eng.Fori(1, G - 1) as t:
                    body(t, False)
                body(G - 1, True)

            def steps(t, last):
                for s in range(1, E + 1):
                    us = [unit(t, s + 2), unit(t, s + 1), unit(t, s)]
                    if last:
                        us = [u if isinstance(u[0], int) and u[0] < G else None for u in us]
                    yield (*us, s)

            block = sbk.enter_context(nc.Block())

            @block.sync
            def _(sp):
                def first():
                    for p in range(2):
                        sp.wait_ge(x1_stored[p], 16 * (G // 2))

                def body(t, last):
                    if not last:
                        load_x1(sp, t + 1)
                    wait(sp, out_done, t)
                    sp.dma_start(resb[:, :, :].rearrange("p b d -> p (b d)"), x1_dram[t]).then_inc(res_loaded_b, 16)
                    sp.wait_ge(out_done, t + 1)
                    sp.dma_start(out_g[t], out_sb[:, :, :]).then_inc(out_stored, 16)

                over_tiles(sp, first, body)
                sp.wait_ge(out_stored, 16 * G)

            @block.gpsimd
            def _(pool):
                def first():
                    p = (G - 1) % 2
                    pool.wait_ge(last_stats_done, 1)
                    nc.gpsimd.tensor_tensor(last_ve[:, :], last_mv[:, :, 1], eps_cols[:, :],
                                            ALU.add).then_inc(last_ve_done, 1)
                    pool.wait_ge(last_ve_done, 1)
                    nc.gpsimd.tensor_tensor(rstd2[p][:, :], last_ve[:, :], minus_half[:, 0:GB],
                                            ALU.pow).then_inc(last_rstd_done, 1)
                    pool.wait_ge(last_rstd_done, 1)
                    nc.gpsimd.tensor_tensor(mean_rstd[:, G - 1, :], last_mv[:, :, 0], rstd2[p][:, :],
                                            ALU.mult).then_inc(mean_rstd_done, 1)
                    pool.wait_ge(bias_out_done, 1)

                def body(t, last):
                    if not last:
                        tile_rstd(pool, t + 1)
                    pool.wait_ge(res_loaded_b, 16 * (t + 1))
                    nc.gpsimd.tensor_tensor(resb[:, :, :], resb[:, :, :],
                                            bias_out[:, None, :].to_broadcast([P, GB, D]),
                                            ALU.add).then_inc(resb_done, 1)

                over_tiles(pool, first, body)

            @block.scalar
            def _(act):
                def relu(u, psum, ready, h, done, row):
                    e = u[1]
                    for c in range(C):
                        act.wait_ge(ready, 2 * uno(u) + c + 1)
                        last = nc.scalar.activation(h[:, c, :], psum[:, c, :], ACT.Relu,
                                                    bias=bn_cols[:, row + 1, C * e + c:C * e + c + 1],
                                                    scale=bn_cols[:, row, C * e + c:C * e + c + 1])
                    last.then_inc(done, 1)

                def relu_1(u):
                    wait(act, lo1_done, uno(u))
                    relu(u, ps_l1, l1_done, h1, r1_done, 0)

                def high_1(u):
                    act.wait_ge(r1_done, uno(u) + 1)
                    wait(act, l2_done, 2 * (uno(u) - 1))
                    nc.scalar.activation(h1_hi[u[1] % 2][:, :, :], h1[:, :, :], ACT.Copy).then_inc(hi1_done, 1)

                def layer_1(u):
                    relu_1(u)
                    high_1(u)

                def relu_2(u):
                    wait(act, m2_done, uno(u))
                    relu(u, ps_l2, l2_done, h2, r2_done, 2)

                def high_2(u):
                    act.wait_ge(m2_done, uno(u) + 1)
                    wait(act, l3_done, uno(u) - 1)
                    nc.scalar.activation(h2_hi[u[1] % 2][:, :, :], h2w[:, :, :], ACT.Copy).then_inc(hi2_done, 1)

                def layer_2(u):
                    relu_2(u)
                    high_2(u)

                def first():
                    layer_1((0, 0))
                    layer_1((0, 1))
                    act.wait_ge(featT_ready, 1)
                    nc.scalar.activation(featT[:, :, :], ps_t[:, 0:D].rearrange("p (c n) -> p c n", c=C),
                                         ACT.Copy, scale=1.0 / B).then_inc(featT_copied, 1)
                    relu_2((0, 0))
                    act.wait_ge(neg_max_done, 1)
                    nc.scalar.activation(e_w[:, :], logits[:, :], ACT.Exp, bias=neg_max[:, :]).then_inc(e_w_done, 1)
                    layer_1((0, 2))
                    act.wait_ge(w_rows_ready, 1)
                    nc.scalar.activation(w_bc[:, :, :], ps_y[:, :, :].rearrange("p b (e n) -> p (b e) n", n=P),
                                         ACT.Copy).then_inc(w_bc_done, 1)
                    high_2((0, 0))
                    act.wait_ge(w_nodeT_ready, 1)
                    nc.scalar.activation(w_nodeT[:, :], ps_t[0:E, 0:P], ACT.Copy).then_inc(w_nodeT_copied, 1)
                    layer_2((0, 1))
                    act.wait_ge(bias_ready, 1)
                    nc.scalar.activation(bias_out[:, :], ps_t[:, T:T + D], ACT.Copy).then_inc(bias_out_done, 1)

                def body(t, last):
                    for u1, u2, u3, s in steps(t, last):
                        if u1:
                            layer_1(u1)
                        if s == E - 3 and not last:
                            wait(act, l1_done, 2 * E * (t + 1))
                            tile_high(act, t + 1, ps_t_x)
                        if u2:
                            layer_2(u2)

                over_tiles(act, first, body)

            @block.vector
            def _(dve):
                def layer_1(u):
                    dve.wait_ge(hi1_done, uno(u) + 1)
                    p = u[1] % 2
                    nc.vector.tensor_tensor(h1_lo[p][:, :, :], h1[:, :, :], h1_hi[p][:, :, :].bitcast(F32),
                                            ALU.subtract).then_inc(lo1_done, 1)

                def layer_2(u):
                    e, p = u[1], u[1] % 2
                    dve.wait_ge(r2_done, uno(u) + 1)
                    wait(dve, lo2_done, uno(u))
                    nc.vector.tensor_tensor(h2w[:, :, :].rearrange("p c (b n) -> p (c b) n", n=N),
                                            h2[:, :, :].rearrange("p c (b n) -> p (c b) n", n=N),
                                            w_bc[:, e:e + 1, :].to_broadcast([P, C * GB, N]),
                                            ALU.mult).then_inc(m2_done, 1)
                    dve.wait_ge(hi2_done, uno(u) + 1)
                    nc.vector.tensor_tensor(h2_lo[p][:, :, :], h2w[:, :, :], h2_hi[p][:, :, :].bitcast(F32),
                                            ALU.subtract).then_inc(lo2_done, 1)

                def out_add(t):
                    dve.wait_ge(l3_done, E * (t + 1))
                    dve.wait_ge(resb_done, t + 1)
                    wait(dve, out_stored, 16 * t)
                    nc.vector.tensor_tensor(out_sb[:, :, :], ps_y[:, :, :], resb[:, :, :],
                                            ALU.add).then_inc(out_done, 1)

                def first():
                    layer_1((0, 0))
                    dve.wait_ge(acc_done, 1)
                    dve.wait_ge(last_rstd_done, 1)
                    add_group((G - 1) % 2)
                    dve.wait_ge(mean_rstd_done, 1)
                    nc.vector.reduce_sum(mean_sum[:, :], mean_rstd[:, :, :].rearrange("p g b -> p (g b)"), AX_X)
                    dve.wait_ge(acc_done, 2)
                    nc.vector.tensor_reduce(feat_sum[:, :], acc[:, :, :].rearrange("p b d -> p d b"), AX_X,
                                            ALU.add).then_inc(feat_sum_done, 1)
                    dve.wait_ge(feat_sum_done, 1)
                    nc.vector.tensor_scalar(feat[:, :], feat_sum[:, :], mean_sum[:, :], None,
                                            ALU.subtract).then_inc(feat_done, 1)
                    layer_1((0, 1))
                    dve.wait_ge(logits_ready, 1)
                    nc.vector.tensor_tensor(logits[:, :], ps_t[:, T:T + E], br_sb[:, :],
                                            ALU.add).then_inc(logits_done, 1)
                    dve.wait_ge(logits_done, 1)
                    nc.vector.tensor_reduce(neg_max[:, :], logits[:, :], AX_X, ALU.max,
                                            negate=True).then_inc(neg_max_done, 1)
                    dve.wait_ge(e_w_done, 1)
                    nc.vector.reduce_sum(e_sum[:, :], e_w[:, :], AX_X).then_inc(e_sum_done, 1)
                    dve.wait_ge(e_sum_done, 1)
                    nc.vector.reciprocal(e_rinv[:, :], e_sum[:, :]).then_inc(e_rinv_done, 1)
                    dve.wait_ge(e_rinv_done, 1)
                    nc.vector.tensor_scalar(w_node[:, :], e_w[:, :], e_rinv[:, :], None,
                                            ALU.mult).then_inc(w_node_done, 1)
                    layer_1((0, 2))
                    dve.wait_ge(w_bc_done, 1)
                    layer_2((0, 0))
                    layer_2((0, 1))

                def body(t, last):
                    for u1, u2, u3, s in steps(t, last):
                        if s == 2 and not last:
                            tile_stats(dve, t + 1)
                            dve.wait_ge(bnst, t + 2)
                        if s == 3 and not last:
                            tile_normalise(dve, t + 1)
                        if s == E:
                            out_add(t)
                        if u1:
                            layer_1(u1)
                        if s == E - 3 and not last:
                            tile_low(dve, t + 1, ps_t_x)
                        if s == 2 and not last:
                            tile_aggregate(t + 1)
                        if u2:
                            layer_2(u2)

                over_tiles(dve, first, body)

            @block.tensor
            def _(pe):
                def layer_1(u):
                    t, e = u
                    if e == 0:
                        pe.wait_ge(xlo_done, t + 1)
                    wait(pe, r1_done, uno(u))
                    for m in range(C):
                        product(ps_l1[:, m, :], e, xT_hi, xT_lo, m, True, True).then_inc(l1_done, 1)

                def layer_2(u):
                    e = u[1]
                    pe.wait_ge(lo1_done, uno(u) + 1)
                    wait(pe, r2_done, uno(u))
                    for m in range(C):
                        product(ps_l2[:, m, :], E + e, h1_hi[e % 2], h1_lo[e % 2], m, True, True).then_inc(l2_done, 1)

                def layer_3(u):
                    t, e = u
                    pe.wait_ge(lo2_done, uno(u) + 1)
                    if e == 0:
                        wait(pe, out_done, t)
                    i, hi, lo = 2 * E + e, h2_hi[e % 2], h2_lo[e % 2]
                    per_bank = T // D
                    for b4 in range(GB):
                        cols = slice(b4 * N, (b4 + 1) * N)
                        terms = [(h, w, c) for c in range(C) for h, w in ((hi, w_hi), (hi, w_lo), (lo, w_hi))]
                        for n, (h, w, c) in enumerate(terms):
                            mm = nc.tensor.matmul(ps_y[:, b4, :], h[:, c, cols], w[:, i, c, :],
                                                  start=(e == 0 and n == 0 and b4 % per_bank == 0),
                                                  stop=(e == E - 1 and n == len(terms) - 1
                                                        and b4 % per_bank == per_bank - 1))
                    mm.then_inc(l3_done, 1)

                def first():
                    layer_1((0, 1))
                    layer_2((0, 0))
                    pe.wait_ge(feat_done, 1)
                    for c in range(C):
                        last = nc.tensor.transpose(ps_t[:, c * P:(c + 1) * P], feat[:, c * P:(c + 1) * P],
                                                   ident[:, :])
                    last.then_inc(featT_ready, 1)
                    pe.wait_ge(featT_copied, 1)
                    for c in range(C):
                        last = nc.tensor.matmul(ps_t[:, T:T + E], featT[:, c, :], wr_sb[:, c, :],
                                                start=(c == 0), stop=(c == C - 1))
                    last.then_inc(logits_ready, 1)
                    layer_1((0, 2))
                    pe.wait_ge(w_node_done, 1)
                    w_rows = ps_y[:, :, :].rearrange("p b (e n) -> p (b e) n", n=P)
                    for e in range(E):
                        last = nc.tensor.matmul(w_rows[:, e, :], w_node[:, e:e + 1].to_broadcast([P, P]),
                                                ident[:, :], start=True, stop=True)
                    last.then_inc(w_rows_ready, 1)
                    nc.tensor.transpose(ps_t[0:E, 0:P], w_node[:, :], ident[:, :]).then_inc(w_nodeT_ready, 1)
                    layer_2((0, 1))
                    pe.wait_ge(w_nodeT_copied, 1)
                    nc.tensor.matmul(ps_t[:, T:T + D], w_nodeT[:, :], bo_sb[:, :], start=True,
                                     stop=True).then_inc(bias_ready, 1)
                    pe.wait_ge(w_bc_done, 1)
                    layer_3((0, 0))

                def body(t, last):
                    for u1, u2, u3, s in steps(t, last):
                        if u1:
                            layer_1(u1)
                        if s == 4 and not last:
                            wait(pe, xlo_done, t + 1)
                            if isinstance(t, int) and t == 0:
                                pe.wait_ge(bias_out_done, 1)
                            tile_transpose(pe, t + 1, ps_t_x)
                        if u2:
                            layer_2(u2)
                        if u3:
                            layer_3(u3)

                over_tiles(pe, first, body)


_INS = ["x", "adj", "L0_gnn_W", "L0_gnn_a", "L0_ffn_Wr", "L0_ffn_br", "L0_ffn_W1", "L0_ffn_b1", "L0_ffn_g1",
        "L0_ffn_be1", "L0_ffn_m1", "L0_ffn_v1", "L0_ffn_W2", "L0_ffn_b2", "L0_ffn_g2", "L0_ffn_be2", "L0_ffn_m2",
        "L0_ffn_v2", "L0_ffn_Wo", "L0_ffn_bo"]


def kernel(**inputs):
    import numpy as _np
    import concourse.bacc as _bacc
    from concourse.bass_utils import run_bass_kernel_spmd as _run

    nc = _bacc.Bacc("TRN2", target_bir_lowering=False, num_devices=1)
    arrays, args = {}, []
    for name in _INS:
        a = _np.ascontiguousarray(inputs[name])
        arrays[f"in_{name}"] = a
        args.append(nc.dram_tensor(f"in_{name}", a.shape, mybir.dt.from_np(a.dtype), kind="ExternalInput").ap())
    out = nc.dram_tensor("out_0", inputs["x"].shape, F32, kind="ExternalOutput").ap()
    adj_ffn(nc, *args, out)
    r = _run(nc, [arrays], core_ids=[0])
    return r.results[0]["out_0"]
```
